# Optimizing a Trainium2 kernel written in Bass

```python
import numpy as np
import jax
import jax.numpy as jnp

def _softmax(x, axis=-1):
    return jax.nn.softmax(x, axis=axis)

def _gelu(x):
    return jax.nn.gelu(x, approximate=True)

def _silu(x):
    return jax.nn.silu(x)

def _sigmoid(x):
    return jax.nn.sigmoid(x)

def _layernorm(x, axis=-1, eps=1e-05):
    m = jnp.mean(x, axis=axis, keepdims=True)
    v = jnp.var(x, axis=axis, keepdims=True)
    return (x - m) / jnp.sqrt(v + eps)

def _scatter_add(tgt, idx, src, axis=0):
    return tgt.at[idx].add(src)

def _segment_sum(src, seg, n):
    return jax.ops.segment_sum(src, seg, n)
kernel_name = 'mk_cond_resid_d2_seqx_r8_54c99b'

def setup_inputs(seed: int=0):
    np.random.seed(seed)
    _w = jnp.asarray

    def _rec_inputs():
        import jax
        import jax.numpy as jnp
        _rk = jax.random.key(seed)
        x = -0.0003929 + 0.9999 * jax.random.normal(jax.random.fold_in(_rk, 1), (64, 32, 512), jnp.float32)
        _lenS = 32 - jax.random.randint(jax.random.fold_in(_rk, 7), (64,), 0, max(1, 32 // 4) + 1, jnp.int32)
        _lenS2 = 32 - jax.random.randint(jax.random.fold_in(_rk, 8), (64,), 0, max(1, 32 // 4) + 1, jnp.int32)
        itok_B_8_3872 = jax.random.randint(jax.random.fold_in(_rk, 11), (64,), 8, 3873, jnp.int32)
        itok_B_2_6 = jax.random.randint(jax.random.fold_in(_rk, 12), (64,), 2, 7, jnp.int32)
        return (x, itok_B_8_3872, itok_B_2_6)
    x, itok_B_8_3872, itok_B_2_6 = _rec_inputs()

    def _L0_cond_setup():
        import math
        import jax, jax.numpy as jnp
        import numpy as np
        H, N, B, L = (32, 64, 16, 512)
        DT_MIN, DT_MAX = (0.001, 0.1)

        def _get_kernel(log_dt, C, log_A_real, A_imag, length):
            Cc = C[..., 0] + 1j * C[..., 1]
            dt = jnp.exp(log_dt)
            A = -jnp.exp(log_A_real) + 1j * A_imag
            dtA = A * dt[:, None]
            P = dtA[:, :, None] * jnp.arange(length, dtype=jnp.float32)
            Cs = Cc * (jnp.exp(dtA) - 1.0) / A
            K = 2.0 * jnp.einsum('hn,hnl->hl', Cs, jnp.exp(P)).real
            return K
        key = jax.random.key(seed)
        ks = jax.random.split(key, 6)
        u = jax.random.normal(ks[0], (B, H, L), dtype=jnp.float32)
        length = jax.random.randint(ks[1], (B,), 0, L)
        log_dt = jax.random.uniform(ks[2], (H,), dtype=jnp.float32) * (math.log(DT_MAX) - math.log(DT_MIN)) + math.log(DT_MIN)
        C = jax.random.normal(ks[3], (H, N, 2), dtype=jnp.float32)
        log_A_real = jnp.log(0.5 * jnp.ones((H, N), dtype=jnp.float32))
        A_imag = math.pi * jnp.broadcast_to(jnp.arange(N, dtype=jnp.float32), (H, N))
        D = jax.random.normal(ks[4], (H,), dtype=jnp.float32)
        return {'u': u, 'length': length, 'log_dt': log_dt, 'C': C, 'log_A_real': log_A_real, 'A_imag': A_imag, 'D': D}
    _L0_cond_all = _L0_cond_setup()
    _L0_cond_in = {k: v for k, v in _L0_cond_all.items() if k in ('log_dt', 'C', 'log_A_real', 'A_imag', 'D')}
    del _L0_cond_all

    def _L1_cond_setup():
        import jax, jax.numpy as jnp
        import numpy as np
        B, N, H, F = (4, 64, 512, 1376)
        L, R, RANK = (1, 16, 16)
        SCALE = 0.5
        key = jax.random.key(seed)
        ks = jax.random.split(key, 12)
        nrm = lambda k, shape, fan: jax.random.normal(k, shape, jnp.float32) * fan ** (-0.5)
        inp = {'x': jax.random.normal(ks[0], (B, N, H), jnp.float32), 'W_gate': nrm(ks[1], (F, H), H), 'W_up': nrm(ks[2], (F, H), H), 'W_down': nrm(ks[3], (H, F), F), 'A_gate': nrm(ks[4], (L, R, RANK, H), H), 'B_gate': nrm(ks[5], (L, R, F, RANK), RANK), 'A_up': nrm(ks[6], (L, R, RANK, H), H), 'B_up': nrm(ks[7], (L, R, F, RANK), RANK), 'A_down': nrm(ks[8], (L, R, RANK, F), F), 'B_down': nrm(ks[9], (L, R, H, RANK), RANK), 'lora_indices': jax.random.randint(ks[10], (B,), 0, R), 'layer_idx': 0}
        return inp
    _L1_cond_all = _L1_cond_setup()
    _L1_cond_in = {k: v for k, v in _L1_cond_all.items() if k in ('W_gate', 'W_up', 'W_down', 'A_gate', 'B_gate', 'A_up', 'B_up', 'A_down', 'B_down')}
    del _L1_cond_all
    return {'x': x, 'itok_B_8_3872': itok_B_8_3872, 'itok_B_2_6': itok_B_2_6, 'L0_cond_log_dt': _L0_cond_in['log_dt'], 'L0_cond_C': _L0_cond_in['C'], 'L0_cond_log_A_real': _L0_cond_in['log_A_real'], 'L0_cond_A_imag': _L0_cond_in['A_imag'], 'L0_cond_D': _L0_cond_in['D'], 'L1_cond_W_gate': _L1_cond_in['W_gate'], 'L1_cond_W_up': _L1_cond_in['W_up'], 'L1_cond_W_down': _L1_cond_in['W_down'], 'L1_cond_A_gate': _L1_cond_in['A_gate'], 'L1_cond_B_gate': _L1_cond_in['B_gate'], 'L1_cond_A_up': _L1_cond_in['A_up'], 'L1_cond_B_up': _L1_cond_in['B_up'], 'L1_cond_A_down': _L1_cond_in['A_down'], 'L1_cond_B_down': _L1_cond_in['B_down']}

def reference(x, itok_B_8_3872, itok_B_2_6, L0_cond_log_dt, L0_cond_C, L0_cond_log_A_real, L0_cond_A_imag, L0_cond_D, L1_cond_W_gate, L1_cond_W_up, L1_cond_W_down, L1_cond_A_gate, L1_cond_B_gate, L1_cond_A_up, L1_cond_B_up, L1_cond_A_down, L1_cond_B_down):
    import jax
    import jax.numpy as jnp

    def _L0_cond_ref(u, length, log_dt, C, log_A_real, A_imag, D):
        import math
        import jax, jax.numpy as jnp
        import numpy as np
        H, N, B, L = (32, 64, 16, 512)
        DT_MIN, DT_MAX = (0.001, 0.1)

        def _get_kernel(log_dt, C, log_A_real, A_imag, length):
            Cc = C[..., 0] + 1j * C[..., 1]
            dt = jnp.exp(log_dt)
            A = -jnp.exp(log_A_real) + 1j * A_imag
            dtA = A * dt[:, None]
            P = dtA[:, :, None] * jnp.arange(length, dtype=jnp.float32)
            Cs = Cc * (jnp.exp(dtA) - 1.0) / A
            K = 2.0 * jnp.einsum('hn,hnl->hl', Cs, jnp.exp(P)).real
            return K
        Bq, Hq, Lq = u.shape
        mask = (jnp.arange(Lq) < length[:, None]).astype(u.dtype)
        u_m = u * mask[:, None, :]
        kernel = _get_kernel(log_dt, C, log_A_real, A_imag, Lq)
        n = 2 * Lq
        k_f = jnp.fft.rfft(kernel, n=n)
        u_f = jnp.fft.rfft(u_m, n=n)
        y = jnp.fft.irfft(u_f * k_f, n=n)[..., :Lq]
        y = y + u_m * D[:, None]
        return y * mask[:, None, :]

    def _L1_cond_ref(x, W_gate, W_up, W_down, A_gate, B_gate, A_up, B_up, A_down, B_down, lora_indices, layer_idx):
        import jax, jax.numpy as jnp
        import numpy as np
        B, N, H, F = (4, 64, 512, 1376)
        L, R, RANK = (1, 16, 16)
        SCALE = 0.5

        def lora_add(base, inp, A, B):
            Ab = A[layer_idx][lora_indices]
            Bb = B[layer_idx][lora_indices]
            t = jnp.einsum('bri,bni->bnr', Ab, inp)
            return base + jnp.einsum('bor,bnr->bno', Bb, t) * SCALE
        gate = lora_add(jnp.einsum('bnh,fh->bnf', x, W_gate), x, A_gate, B_gate)
        up = lora_add(jnp.einsum('bnh,fh->bnf', x, W_up), x, A_up, B_up)
        act = jax.nn.silu(gate) * up
        down = lora_add(jnp.einsum('bnf,hf->bnh', act, W_down), act, A_down, B_down)
        return down
    x = x + _L0_cond_ref(x, itok_B_8_3872, L0_cond_log_dt, L0_cond_C, L0_cond_log_A_real, L0_cond_A_imag, L0_cond_D)
    x = x + _L1_cond_ref(x, L1_cond_W_gate, L1_cond_W_up, L1_cond_W_down, L1_cond_A_gate, L1_cond_B_gate, L1_cond_A_up, L1_cond_B_up, L1_cond_A_down, L1_cond_B_down, itok_B_2_6, 0)
    return x

_drawn_inputs = setup_inputs


def setup_inputs(seed=0):
    import zlib

    import numpy as np

    out = dict(_drawn_inputs(seed))
    spreads = {'L0_cond_log_A_real': (-0.6931471824645996, 0.2)}
    factors = {}
    for name, (base, spread) in spreads.items():
        noise = np.random.default_rng([zlib.crc32(name.encode()), seed]).standard_normal(out[name].shape)
        drawn = base * np.exp(spread * noise) if base else spread * noise
        out[name] = jnp.asarray(drawn.astype(out[name].dtype))
    for name, factor in factors.items():
        out[name] = (out[name] * factor).astype(out[name].dtype)
    return out
```

```python
from contextlib import ExitStack

import concourse.bass as bass
from concourse import mybir

F32 = mybir.dt.float32
F32R = mybir.dt.float32r
I32 = mybir.dt.int32
ALU = mybir.AluOpType
ACT = mybir.ActivationFunctionType

P = 128
NB, NH, NL = 64, 32, 512
KB = NL // P
NM = 64
NF = 1376
FB = -(-NF // P)
FLAST = NF - (FB - 1) * P
R = 16
BT = 4
NT = NB // BT
LR = BT * R
CH = [(0, 512), (512, 512), (1024, NF - 1024)]
NC = len(CH)
BLK = [(0, 4), (4, 4), (8, 3)]
WG = 2 * NF
BW = WG + NL
AW = KB * 2 * R + FB * R
DA_W = 288
DB_W = NL - DA_W
PA, PB = 32, 16
HG = 8
NG = NH // HG
LOG2E, LN2_HI = 1.4426950408889634, 0.693359375
LN2_LO = 0.6931471805599453 - LN2_HI
PI = 3.141592653589793
PI_HI = 3.140625
PI_LO = PI - PI_HI
MAGIC = 12582912.0
ABS_BITS = 0x7FFFFFFF
SCALE = 0.5
N_PRM = 6


def chunk_col(c, up):
    return 2 * CH[c][0] + up * CH[c][1]


def program(nc, xT, xr, wgu, wd, atab, btab, prm, lens, idx, out):
    top = ExitStack()
    with top:
        def sem(name):
            return top.enter_context(nc.semaphore(name))

        def sb(scope, name, shape, dt=F32):
            return scope.enter_context(nc.sbuf_tensor(name, shape, dt))

        kpad = nc.dram_tensor("kpad", (NH, P + NL), F32, kind="Internal")

        w_hi = sb(top, "w_hi", [P, KB, WG], F32R)
        w_lo = sb(top, "w_lo", [P, KB, WG], F32R)
        wd_hi = sb(top, "wd_hi", [P, FB, NL + LR], F32R)
        wd_lo = sb(top, "wd_lo", [P, FB, NL + LR], F32R)
        x = sb(top, "x", [P, NH, KB, NB])
        ident = sb(top, "ident", [P, P])
        amask = sb(top, "amask", [P, NH, BT])
        amask_t = sb(top, "amask_t", [P, LR])
        idx_sb = sb(top, "idx_sb", [1, NB], I32)

        pa = ExitStack()
        th = sb(pa, "th", [P, 2, HG, PA + PB])
        rr = sb(pa, "rr", [P, 2, HG, PA + PB])
        ab = sb(pa, "ab", [P, 2, HG, PA + PB])
        e1 = sb(pa, "e1", [P, 2, HG, PA + PB])
        e2 = sb(pa, "e2", [P, 2, HG, PA])
        with ExitStack() as pk:
            gg = sb(pk, "gg", [P, NG, HG, PA + PB])
            small = sb(pk, "small", [P, 28, NH])
            prm_sb = sb(pk, "prm_sb", [P, N_PRM, NH])
            lvec = sb(pk, "lvec", [P, PA + PB])
            sgn = sb(pk, "sgn", [P, 1])
            half_pi = sb(pk, "half_pi", [P, 1])
            zeros = sb(pk, "zeros", [NH, P])
        um = sb(pa, "um", [P, 4, 2 * KB * NB])
        cv = sb(pa, "cv", [P, 2, 2 * KB * NB])
        k_sb = sb(pa, "k_sb", [PA, NG, HG, PB])
        len_i = sb(pa, "len_i", [P, NB], I32)
        len_f = sb(pa, "len_f", [P, NB])
        lcol = sb(pa, "lcol", [P, 2, KB])
        lmask = sb(pa, "lmask", [P, 2, KB, NB])
        toep = sb(pa, "toep", [P, 2, 2, NL])
        stage = sb(pa, "stage", [P, 2, 2 * 512])
        pa.close()

        b_raw = sb(top, "b_raw", [LR, 2, 2 * 512])
        a_raw = sb(top, "a_raw", [P, BT, AW])
        a_gu = sb(top, "a_gu", [P, KB * 2, BT, R])
        bd_raw = sb(top, "bd_raw", [LR, NL])
        b_spl = sb(top, "b_spl", [P, 2, 512], F32R)
        bd_spl = sb(top, "bd_spl", [P, NL], F32R)
        xt = sb(top, "xt", [P, KB, P])
        x_hi = sb(top, "x_hi", [P, 2, KB, P], F32R)
        x_lo = sb(top, "x_lo", [P, 2, KB, P], F32R)
        h_act = sb(top, "h_act", [P, 2, 512])
        ht_hi = sb(top, "ht_hi", [P, FB, P], F32R)
        ht_lo = sb(top, "ht_lo", [P, FB, P], F32R)
        y_sb = sb(top, "y_sb", [P, NL])
        t_m = sb(top, "t_m", [P, NH, BT])
        t_hi = sb(top, "t_hi", [P, 2, P], F32R)
        t_lo = sb(top, "t_lo", [P, 2, P], F32R)
        td_m = sb(top, "td_m", [P, 2, LR])
        td_hi = sb(top, "td_hi", [P, P], F32R)
        td_lo = sb(top, "td_lo", [P, P], F32R)

        ps_g = [top.enter_context(nc.psum_tensor(f"ps_g{i}", [P, 512], F32)) for i in range(2)]
        ps_u = [top.enter_context(nc.psum_tensor(f"ps_u{i}", [P, 512], F32)) for i in range(2)]
        ps_da = top.enter_context(nc.psum_tensor("ps_da", [P, 512], F32))
        ps_db = top.enter_context(nc.psum_tensor("ps_db", [P, 512], F32))
        ps_x = [top.enter_context(nc.psum_tensor(f"ps_x{i}", [P, 512], F32)) for i in range(2)]
        ps_k = [ps_da, ps_db]
        ps_c = [ps_g[0], ps_g[1]]

        prm_in, len_in, x_in, idx_in = sem("prm_in"), sem("len_in"), sem("x_in"), sem("idx_in")
        stage_in = [sem("stage_in0"), sem("stage_in1")]
        stage_hi, stage_lo = sem("stage_hi"), sem("stage_lo")
        consts, ident_s, amask_ok, amask_ps, amaskt_ok = (sem("consts"), sem("ident_s"), sem("amask_ok"), sem("amask_ps"),
                                                 sem("amaskt_ok"))
        steps = sem("steps")
        logmag, mag_done, trig_in, trig_done = sem("logmag"), sem("mag_done"), sem("trig_in"), sem("trig_done")
        ang_in, ang_out, tab_ready = sem("ang_in"), sem("ang_out"), sem("tab_ready")
        k_ps, k_ready, k_out, zero_out = sem("k_ps"), sem("k_ready"), sem("k_out"), sem("zero_out")
        toep_in = [sem("toep_in0"), sem("toep_in1")]
        um_in = [sem(f"um_in{i}") for i in range(4)]
        um_ready, conv_ps, conv_sb, x1_ready = sem("um_ready"), sem("conv_ps"), sem("conv_sb"), sem("x1_ready")
        a_in = sem("a_in")
        ag_ok = sem("ag_ok")
        b_in = [sem("b_in0"), sem("b_in1")]
        bd_in = sem("bd_in")
        b_hi, b_lo = sem("b_hi"), sem("b_lo")
        bd_hi, bd_lo = sem("bd_hi"), sem("bd_lo")
        ad_hi, ad_lo = sem("ad_hi"), sem("ad_lo")
        xt_ok, xhi_ok, xlo_ok = sem("xt_ok"), sem("xhi_ok"), sem("xlo_ok")
        a_ps, tm_ok, thi_ok, tlo_ok = sem("a_ps"), sem("tm_ok"), sem("thi_ok"), sem("tlo_ok")
        g_ps, u_ps, silu_ok, act_ok = sem("g_ps"), sem("u_ps"), sem("silu_ok"), sem("act_ok")
        ht_ps, hthi_ok, htlo_ok = sem("ht_ps"), sem("hthi_ok"), sem("htlo_ok")
        res_ps, res_ok = sem("res_ps"), sem("res_ok")
        down_ps, td_ok, td_ps, tdhi_ok, tdlo_ok = (sem("down_ps"), sem("td_ok"), sem("td_ps"), sem("tdhi_ok"),
                                                   sem("tdlo_ok"))
        y_ps, y_ok, y_out = sem("y_ps"), sem("y_ok"), sem("y_out")

        def wait(eng, s, v):
            if not isinstance(v, int) or v > 0:
                eng.wait_ge(s, v)

        def tiles(eng, body):
            body(0, 0, True, False)
            with eng.Fori(0, NT // 2 - 1) as a:
                body(a, 1, False, False)
                body(a + 1, 0, False, False)
            body(NT // 2 - 1, 1, False, True)

        def chunk_uses(a, q, c):
            return NC * a + (NC * q + c) // 2

        pieces = []
        for kb in range(KB):
            for c in range(NC):
                cols = slice(chunk_col(c, 0), chunk_col(c, 0) + 2 * CH[c][1])
                pieces.append((wgu[kb * P:(kb + 1) * P, cols], w_hi[:, kb, cols], w_lo[:, kb, cols], P, (2 * CH[c][1],)))
        for f0 in range(0, FB - 1, 2):
            pieces.append((wd[f0 * P:(f0 + 2) * P, :].rearrange("(g p) n -> p g n", p=P),
                           wd_hi[:, f0:f0 + 2, 0:NL], wd_lo[:, f0:f0 + 2, 0:NL], P, (2, NL)))
        pieces.append((wd[(FB - 1) * P:NF, :], wd_hi[0:FLAST, FB - 1, 0:NL], wd_lo[0:FLAST, FB - 1, 0:NL], FLAST, (NL,)))

        def staged(n):
            shape = pieces[n][4]
            size = shape[0] * (shape[1] if len(shape) > 1 else 1)
            v = stage[0:pieces[n][3], n % 2, 0:size]
            return v.rearrange("p (g n) -> p g n", g=2) if len(shape) > 1 else v

        block = top.enter_context(nc.Block())

        @block.sync
        def _(sp):
            def load_piece(n):
                wait(sp, stage_lo, n - 1)
                sp.dma_start(staged(n), pieces[n][0]).then_inc(stage_in[n % 2], 16)

            sp.dma_start(prm_sb[:, :, :], prm.rearrange("p (a h) -> p a h", a=N_PRM)).then_inc(prm_in, 16)
            sp.dma_start(len_i[:, :], lens.partition_broadcast(P)).then_inc(len_in, 16)
            sp.dma_start(idx_sb[0:1, :], idx.partition_broadcast(1)).then_inc(idx_in, 16)
            sp.wait_ge(consts, 1)
            sp.dma_start(kpad.ap()[:, 0:P], zeros[:, :]).then_inc(zero_out, 16)
            for n in range(2):
                load_piece(n)
            sp.dma_start(x[:, :, :, :].rearrange("p h k b -> p (h k b)"), xT).then_inc(x_in, 16)
            for n in range(2, 6):
                load_piece(n)
            for g in range(NG):
                for n in range(3 * g + 6, 3 * g + 9):
                    load_piece(n)
                sp.wait_ge(k_ready, g + 1)
                dst = bass.AP(tensor=kpad, offset=g * HG * (P + NL) + P, ap=[[PB, PA], [P + NL, HG], [1, PB]])
                sp.dma_start(dst, k_sb[:, g, :, :]).then_inc(k_out, 16)
            sp.wait_ge(zero_out, 16)
            sp.wait_ge(k_out, 16 * NG)

            def load_toep(pair, slot, first):
                if not first:
                    sp.wait_ge(conv_ps, pair - 1)
                src = bass.AP(tensor=kpad, offset=pair * (2 * (P + NL)) + 1, ap=[[1, P], [P + NL, 2], [1, NL]])
                sp.dma_start(toep[:, slot, :, :], src).then_inc(toep_in[slot], 16)

            def load_um(pair, slot, first):
                if not first:
                    sp.wait_ge(conv_ps, pair - 3)
                sp.dma_start(um[:, slot, :], xr[bass.ds(pair * P, P), :]).then_inc(um_in[slot], 16)

            for pair in range(4):
                load_toep(pair, pair % 2, pair < 2)
                load_um(pair, pair, True)
            with sp.Fori(1, NH // 8) as j:
                for i in range(4):
                    load_toep(4 * j + i, i % 2, False)
                    load_um(4 * j + i, i, False)

            def indices(a, q):
                return [sp.value_load(idx_sb[0:1, bass.ds((2 * a + q) * BT + b, 1)], min_val=0, max_val=15)
                        for b in range(BT)]

            def load_a(a, q, ids):
                wait(sp, ag_ok, 2 * a + q)
                wait(sp, ad_lo, 2 * a + q)
                for b in range(BT):
                    src = atab[bass.ds(ids[b], 1), :, :].rearrange("a p n -> (a p) n")
                    sp.dma_start(a_raw[:, b, :], src).then_inc(a_in, 16)

            def load_b(a, q, c, ids):
                n = NC * (2 * a + q) + c
                wait(sp, b_lo, 2 * n - 2)
                slot, w = (NC * q + c) % 2, 2 * CH[c][1]
                for b in range(BT):
                    src = btab[bass.ds(ids[b], 1), :, chunk_col(c, 0):chunk_col(c, 0) + w].rearrange("a r n -> (a r) n")
                    sp.dma_start(b_raw[b * R:(b + 1) * R, slot, 0:w], src).then_inc(b_in[slot], 16)

            def load_bd(a, q, ids):
                wait(sp, bd_lo, 2 * a + q)
                for b in range(BT):
                    src = btab[bass.ds(ids[b], 1), :, WG:BW].rearrange("a r n -> (a r) n")
                    sp.dma_start(bd_raw[b * R:(b + 1) * R, :], src).then_inc(bd_in, 16)

            def store(a, q):
                t = 2 * a + q
                sp.wait_ge(y_ok, 2 * t + 2)
                sp.dma_start(out[bass.ds(t * P, P), :], y_sb[:, :]).then_inc(y_out, 16)

            sp.wait_ge(idx_in, 16)
            sp.wait_ge(k_ps, NG)
            sp.wait_ge(k_out, 16 * NG)
            ids0 = indices(0, 0)
            load_a(0, 0, ids0)
            load_b(0, 0, 0, ids0)
            load_b(0, 0, 1, ids0)
            load_bd(0, 0, ids0)

            def body(a, q, first, last):
                load_b(a, q, 2, indices(a, q))
                na, nq = (a, 1) if q == 0 else (a + 1, 0)
                if not last:
                    ids = indices(na, nq)
                    load_b(na, nq, 0, ids)
                if not first:
                    store(*((a, 0) if q == 1 else (a - 1, 1)))
                if not last:
                    load_a(na, nq, ids)
                    load_bd(na, nq, ids)
                    load_b(na, nq, 1, ids)

            tiles(sp, body)
            store(NT // 2 - 1, 1)
            sp.wait_ge(y_out, 16 * NT)

        @block.gpsimd
        def _(pool):
            nc.gpsimd.memset(zeros[:, :], 0.0).then_inc(consts, 1)
            nc.gpsimd.iota(lvec[:, 0:PA], pattern=[[PB, PA]], base=0, channel_multiplier=0,
                           allow_small_or_imprecise_dtypes=True).then_inc(consts, 1)
            nc.gpsimd.iota(lvec[:, PA:PA + PB], pattern=[[1, PB]], base=0, channel_multiplier=0,
                           allow_small_or_imprecise_dtypes=True).then_inc(consts, 1)
            for i in range(2):
                nc.gpsimd.iota(lcol[:, i, :], pattern=[[P, KB]], base=(P - 1, 0)[i], channel_multiplier=(-1, 1)[i],
                               allow_small_or_imprecise_dtypes=True).then_inc(consts, 1)
            nc.gpsimd.memset(half_pi[:, :], PI / 2).then_inc(consts, 1)
            nc.gpsimd.memset(ident[:, :], 0.0).then_inc(ident_s, 1)
            pool.wait_ge(ident_s, 1)
            nc.gpsimd.affine_select(out=ident[:, :], in_=ident[:, :], compare_op=ALU.not_equal, fill=1.0, base=0,
                                    pattern=[[-1, P]], channel_multiplier=1).then_inc(ident_s, 1)
            nc.gpsimd.memset(amask[:, :, :], SCALE).then_inc(amask_ok, 1)
            pool.wait_ge(amask_ok, 1)
            for h in range(2):
                v = amask[h * LR:(h + 1) * LR, :, :]
                nc.gpsimd.affine_select(out=v, in_=v, compare_op=ALU.is_ge, fill=0.0, base=0,
                                        pattern=[[0, NH], [-R, BT]], channel_multiplier=1).then_inc(amask_ok, 1)
            pool.wait_ge(amask_ok, 3)
            for h in range(2):
                v = amask[h * LR:(h + 1) * LR, :, :]
                nc.gpsimd.affine_select(out=v, in_=v, compare_op=ALU.is_ge, fill=0.0, base=R - 1,
                                        pattern=[[0, NH], [R, BT]], channel_multiplier=-1).then_inc(amask_ok, 1)
            pool.wait_ge(amask_ok, 5)

            def split_lo(n):
                pool.wait_ge(stage_hi, n + 1)
                nc.gpsimd.tensor_tensor(pieces[n][2], staged(n), pieces[n][1].bitcast(F32),
                                        ALU.subtract).then_inc(stage_lo, 1)

            for n in range(len(pieces)):
                split_lo(n)

            def add_conv(pair, slot):
                pool.wait_ge(conv_sb, pair + 1)
                v = x[:, bass.ds(2 * pair, 2), :, :].rearrange("p h k b -> p (h k b)")
                nc.gpsimd.tensor_tensor(v, v, cv[:, slot, :], ALU.add).then_inc(x1_ready, 1)

            with pool.Fori(0, NH // 4) as j:
                add_conv(2 * j, 0)
                add_conv(2 * j + 1, 1)

            def tokens(a, q):
                t = 2 * a + q
                wait(pool, res_ps, t)
                wait(pool, xlo_ok, t)
                wait(pool, a_ps, t)
                pool.wait_ge(a_in, 16 * BT * (t + 1))
                pool.wait_ge(x1_ready, NH // 2)
                nc.gpsimd.tensor_copy(xt[:, :, :].rearrange("p k (h b) -> p k h b", b=BT),
                                      x[:, :, :, bass.ds(t * BT, BT)].rearrange("p h k b -> p k h b")).then_inc(xt_ok, 1)
                src = a_raw[:, :, 0:KB * 2 * R].rearrange("p b (k r) -> p k b r", r=R)
                nc.gpsimd.tensor_copy(a_gu[:, :, :, :], src).then_inc(ag_ok, 1)

            tokens(0, 0)

            def body(a, q, first, last):
                if not last:
                    tokens(*((a, 1) if q == 0 else (a + 1, 0)))

            tiles(pool, body)

        @block.scalar
        def _(act):
            def split_hi(n):
                act.wait_ge(stage_in[n % 2], 16 * (n // 2 + 1))
                nc.scalar.copy(pieces[n][1], staged(n)).then_inc(stage_hi, 1)

            act.wait_ge(consts, 6)
            act.wait_ge(ang_in, 1)
            nc.scalar.activation(small[:, 16, :], small[:, 14, :], ACT.Sin).then_inc(ang_out, 1)
            nc.scalar.activation(small[:, 17, :], small[:, 15, :], ACT.Sin, bias=half_pi[:, :],
                                 scale=-1.0).then_inc(ang_out, 1)
            act.wait_ge(logmag, NG)
            nc.scalar.activation(gg[:, :, :, :], gg[:, :, :, :], ACT.Exp).then_inc(mag_done, 1)
            for n in range(2):
                split_hi(n)
            for g in range(NG):
                s = g % 2
                act.wait_ge(trig_in, g + 1)
                if g >= 2:
                    act.wait_ge(k_ps, g - 1)
                nc.scalar.activation(e1[0:NM, s, :, :], ab[0:NM, s, :, :], ACT.Sin, bias=half_pi[0:NM, :],
                                     scale=-1.0).then_inc(trig_done, 1)
                nc.scalar.activation(e1[NM:P, s, :, :], rr[NM:P, s, :, :], ACT.Sin).then_inc(trig_done, 1)
                nc.scalar.activation(e2[0:NM, s, :, :], rr[0:NM, s, :, 0:PA], ACT.Sin).then_inc(trig_done, 1)
                nc.scalar.activation(e2[NM:P, s, :, :], ab[NM:P, s, :, 0:PA], ACT.Sin, bias=half_pi[NM:P, :],
                                     scale=-1.0).then_inc(trig_done, 1)
                for n in range(4 * g + 2, 4 * g + 6):
                    split_hi(n)

            def x_hi_part(a, q, first):
                t = 2 * a + q
                act.wait_ge(xt_ok, t + 1)
                if first:
                    act.wait_ge(conv_ps, NH // 2)
                    act.wait_ge(stage_lo, len(pieces))
                else:
                    wait(act, u_ps, NC * (t - 1))
                nc.scalar.copy(x_hi[:, q, :, :], xt[:, :, :]).then_inc(xhi_ok, 1)

            def b_hi_part(a, q, c, up):
                n = NC * (2 * a + q) + c
                slot, w = (NC * q + c) % 2, CH[c][1]
                if up == 0:
                    act.wait_ge(b_in[slot], 16 * BT * (chunk_uses(a, q, c) + 1))
                wait(act, u_ps if up else g_ps, n)
                nc.scalar.copy(b_spl[0:LR, up, 0:w], b_raw[:, slot, up * w:(up + 1) * w]).then_inc(b_hi, 1)

            def body(a, q, first, last):
                t = 2 * a + q
                na, nq = (a, 1) if q == 0 else (a + 1, 0)
                act.wait_ge(tm_ok, t + 1)
                wait(act, u_ps, NC * t)
                for up in range(2):
                    src = t_m[up * LR:(up + 1) * LR, :, :].rearrange("p h b -> p (h b)")
                    nc.scalar.copy(t_hi[0:LR, up, :], src).then_inc(thi_ok, 1)
                    nc.scalar.copy(t_hi[LR:P, up, :], src).then_inc(thi_ok, 1)
                if not first:
                    td_hi_part(t - 1)

                def silu(c):
                    n = NC * t + c
                    act.wait_ge(g_ps, n + 1)
                    wait(act, ht_ps, n - 1)
                    s, w = (NC * q + c) % 2, CH[c][1]
                    nc.scalar.activation(h_act[:, s, 0:w], ps_g[s][:, 0:w], ACT.Silu).then_inc(silu_ok, 1)

                def ht_hi_part(c):
                    act.wait_ge(ht_ps, NC * t + c + 1)
                    if c == 0:
                        wait(act, down_ps, t)
                    evacuate(c, ht_hi, c != 0 and 1 or 0)

                def evacuate(c, dst, bank):
                    f0, nf = BLK[c]
                    bank = [0, 1, 1][c]
                    if c < NC - 1:
                        nc.scalar.copy(dst[:, f0:f0 + nf, :],
                                       ps_x[bank][:, 0:nf * P].rearrange("p (f t) -> p f t", t=P)).then_inc(hthi_ok, 1)
                    else:
                        nc.scalar.copy(dst[:, f0:f0 + nf - 1, :],
                                       ps_x[bank][:, 0:(nf - 1) * P].rearrange("p (f t) -> p f t", t=P)).then_inc(hthi_ok, 1)
                        nc.scalar.copy(dst[0:FLAST, f0 + nf - 1, :],
                                       ps_x[bank][0:FLAST, (nf - 1) * P:nf * P]).then_inc(hthi_ok, 1)

                act.wait_ge(a_in, 16 * BT * (t + 1))
                wait(act, down_ps, t)
                ad = a_raw[:, :, KB * 2 * R:AW].rearrange("p b (f r) -> p f b r", r=R)
                nc.scalar.copy(wd_hi[:, :, NL:NL + LR].rearrange("p f (b r) -> p f b r", r=R), ad).then_inc(ad_hi, 1)
                silu(0)
                b_hi_part(a, q, 1, 0)
                b_hi_part(a, q, 1, 1)
                act.wait_ge(bd_in, 16 * BT * (t + 1))
                wait(act, y_ps, t)
                nc.scalar.copy(bd_spl[0:LR, :], bd_raw[:, :]).then_inc(bd_hi, 1)
                silu(1)
                b_hi_part(a, q, 2, 0)
                b_hi_part(a, q, 2, 1)
                ht_hi_part(0)
                silu(2)
                if not last:
                    b_hi_part(na, nq, 0, 0)
                    b_hi_part(na, nq, 0, 1)
                ht_hi_part(1)
                act.wait_ge(res_ps, t + 1)
                wait(act, y_out, 16 * t)
                nc.scalar.copy(y_sb[:, :], ps_x[0][:, :]).then_inc(res_ok, 1)
                if not last:
                    x_hi_part(na, nq, False)
                ht_hi_part(2)

            def td_hi_part(t):
                act.wait_ge(td_ps, t + 1)
                wait(act, y_ps, t)
                nc.scalar.copy(td_hi[:, :], ps_x[1][:, 0:P]).then_inc(tdhi_ok, 1)

            x_hi_part(0, 0, True)
            b_hi_part(0, 0, 0, 0)
            b_hi_part(0, 0, 0, 1)
            tiles(act, body)
            td_hi_part(NT - 1)

        @block.vector
        def _(dve):
            count = [0]

            def step(ins, now=True):
                count[0] += 1
                ins.then_inc(steps, 1)
                if now:
                    dve.wait_ge(steps, count[0])

            def sm(i, n=1):
                return small[:, i:i + n, :]

            V = nc.vector

            def exp_parts(src, at, n):
                q_, s_, r_, k_ = sm(at, n), sm(at + n, n), sm(at + 2 * n, n), sm(at + 3 * n, n)
                step(V.tensor_scalar(r_, src, 88.0, -87.0, ALU.min, ALU.max))
                step(V.tensor_scalar(s_, r_, LOG2E, MAGIC + 127.0, ALU.mult, ALU.add))
                step(V.tensor_scalar(k_, s_, MAGIC + 127.0, None, ALU.subtract))
                step(V.tensor_scalar(s_.bitcast(I32), s_.bitcast(I32), 23, None, ALU.logical_shift_left))
                step(V.scalar_tensor_tensor(out=r_, in0=k_, scalar=-LN2_HI, in1=r_, op0=ALU.mult, op1=ALU.add))
                step(V.scalar_tensor_tensor(out=r_, in0=k_, scalar=-LN2_LO, in1=r_, op0=ALU.mult, op1=ALU.add))
                step(V.tensor_scalar(q_, r_, 1 / 5040, None, ALU.mult))
                for c in (1 / 720, 1 / 120, 1 / 24, 1 / 6, 1 / 2, 1.0):
                    step(V.scalar_tensor_tensor(out=q_, in0=q_, scalar=c, in1=r_, op0=ALU.add, op1=ALU.mult))
                return q_, s_

            def stt(o, i, i0, s, i1, op0, op1):
                step(V.scalar_tensor_tensor(out=sm(o), in0=sm(i0), scalar=s, in1=i1, op0=op0, op1=op1))

            step(V.memset(sgn[0:NM, :], 1.0), False)
            step(V.memset(sgn[NM:P, :], -1.0), False)
            prm_ = lambda i, n=1: prm_sb[:, i:i + n, :]
            dve.wait_ge(prm_in, 16)
            q_, s_ = exp_parts(prm_(0, 2), 0, 2)
            step(V.scalar_tensor_tensor(out=sm(8, 2), in0=q_, scalar=1.0, in1=s_, op0=ALU.add, op1=ALU.mult))
            DT, NAR, DAR, DAI = 8, 9, 10, 11
            step(V.scalar_tensor_tensor(out=sm(DAR), in0=sm(NAR), scalar=-1.0, in1=sm(DT), op0=ALU.mult, op1=ALU.mult))
            step(V.tensor_tensor(sm(DAI), prm_(2), sm(DT), ALU.mult))
            dve.wait_ge(consts, 6)
            step(V.tensor_scalar(sm(12), sm(DAI), 0.5, None, ALU.mult))
            step(V.tensor_scalar(sm(13), sm(12), 1 / PI, MAGIC, ALU.mult, ALU.add))
            step(V.tensor_scalar(sm(13), sm(13), MAGIC, None, ALU.subtract))
            step(V.scalar_tensor_tensor(out=sm(14), in0=sm(13), scalar=-PI_HI, in1=sm(12), op0=ALU.mult, op1=ALU.add))
            step(V.scalar_tensor_tensor(out=sm(14), in0=sm(13), scalar=-PI_LO, in1=sm(14), op0=ALU.mult, op1=ALU.add))
            V.tensor_scalar(sm(15).bitcast(I32), sm(14).bitcast(I32), ABS_BITS, None, ALU.bitwise_and).then_inc(ang_in, 1)

            def phases(g):
                s = g % 2
                hs = slice(g * HG, (g + 1) * HG)
                shape = [P, HG, PA + PB]
                lv = lvec[:, :].unsqueeze(1).broadcast_to(shape)
                dai = small[:, DAI, hs].unsqueeze(2).broadcast_to(shape)
                t_, r_, a_ = th[:, s], rr[:, s], ab[:, s]
                step(V.tensor_tensor(r_, dai, lv, ALU.mult))
                step(V.tensor_scalar(t_, r_, 1 / PI, MAGIC, ALU.mult, ALU.add))
                step(V.tensor_scalar(a_, t_, MAGIC, None, ALU.subtract))
                step(V.scalar_tensor_tensor(out=r_, in0=a_, scalar=-PI_HI, in1=r_, op0=ALU.mult, op1=ALU.add))
                step(V.scalar_tensor_tensor(out=r_, in0=a_, scalar=-PI_LO, in1=r_, op0=ALU.mult, op1=ALU.add))
                V.tensor_scalar(a_.bitcast(I32), r_.bitcast(I32), ABS_BITS, None, ALU.bitwise_and).then_inc(trig_in, 1)

            for g in range(NG):
                shape = [P, HG, PA + PB]
                V.tensor_tensor(gg[:, g], small[:, DAR, g * HG:(g + 1) * HG].unsqueeze(2).broadcast_to(shape),
                                lvec[:, :].unsqueeze(1).broadcast_to(shape), ALU.mult).then_inc(logmag, 1)
            phases(0)
            phases(1)
            q_, s_ = exp_parts(sm(DAR), 0, 1)
            step(V.tensor_tensor(sm(4), q_, s_, ALU.mult))
            step(V.scalar_tensor_tensor(out=sm(4), in0=s_, scalar=-1.0, in1=sm(4), op0=ALU.add, op1=ALU.add))
            dve.wait_ge(ang_out, 2)
            SI, CO, EM = 16, 17, 4
            step(V.tensor_tensor(sm(19), sm(SI), sm(SI), ALU.mult))
            step(V.tensor_scalar(sm(20), sm(19), -2.0, 1.0, ALU.mult, ALU.add))
            step(V.tensor_tensor(sm(20), sm(20), sm(EM), ALU.mult))
            step(V.scalar_tensor_tensor(out=sm(20), in0=sm(19), scalar=-2.0, in1=sm(20), op0=ALU.mult, op1=ALU.add))
            step(V.tensor_tensor(sm(21), sm(SI), sm(CO), ALU.mult))
            step(V.tensor_scalar(sm(21), sm(21), 2.0, None, ALU.mult))
            step(V.scalar_tensor_tensor(out=sm(21), in0=sm(EM), scalar=1.0, in1=sm(21), op0=ALU.add, op1=ALU.mult))
            XR, YI = 20, 21
            step(V.tensor_tensor(sm(22), sm(NAR), sm(NAR), ALU.mult), False)
            step(V.tensor_tensor(sm(23), prm_(2), prm_(2), ALU.mult))
            step(V.tensor_tensor(sm(22), sm(22), sm(23), ALU.add))
            step(V.reciprocal(sm(22), sm(22)))
            step(V.tensor_tensor(sm(23), sm(YI), prm_(2), ALU.mult), False)
            step(V.tensor_tensor(sm(24), sm(XR), sm(NAR), ALU.mult))
            step(V.tensor_tensor(sm(23), sm(23), sm(24), ALU.subtract))
            step(V.tensor_tensor(sm(23), sm(23), sm(22), ALU.mult), False)
            step(V.tensor_tensor(sm(24), sm(XR), prm_(2), ALU.mult), False)
            step(V.tensor_tensor(sm(25), sm(YI), sm(NAR), ALU.mult))
            step(V.scalar_tensor_tensor(out=sm(24), in0=sm(24), scalar=-1.0, in1=sm(25), op0=ALU.mult, op1=ALU.subtract))
            step(V.tensor_tensor(sm(24), sm(24), sm(22), ALU.mult))
            step(V.tensor_tensor(sm(25), prm_(3), sm(23), ALU.mult), False)
            step(V.tensor_tensor(sm(26), prm_(4), sm(24), ALU.mult))
            step(V.tensor_tensor(sm(25), sm(25), sm(26), ALU.subtract))
            step(V.tensor_tensor(sm(26), prm_(3), sm(24), ALU.mult), False)
            step(V.tensor_tensor(sm(27), prm_(4), sm(23), ALU.mult))
            step(V.tensor_tensor(sm(26), sm(26), sm(27), ALU.add))
            step(V.tensor_scalar(sm(25), sm(25), sgn[:, :], 2.0, ALU.mult, ALU.mult))
            step(V.tensor_scalar(sm(26), sm(26), -2.0, None, ALU.mult))
            dve.wait_ge(len_in, 16)
            step(V.tensor_copy(len_f[:, :], len_i[:, :]))
            for i in range(2):
                for kb in range(KB):
                    step(V.tensor_scalar(lmask[:, i, kb, :], len_f[:, :], lcol[:, i, kb:kb + 1], None, ALU.is_gt), False)
            dve.wait_ge(steps, count[0])
            mask_in, mask_out = (lmask[:, i, :, :].rearrange("p k b -> p (k b)").unsqueeze(1).broadcast_to([P, 2, KB * NB])
                                 for i in range(2))

            def taps(g):
                dve.wait_ge(k_ps, g + 1)
                step(V.tensor_copy(k_sb[:, g, :, :], ps_k[g % 2][0:PA, 0:HG * PB].rearrange("a (h b) -> a h b", b=PB)))
                V.tensor_tensor(k_sb[0:1, g, :, 0], k_sb[0:1, g, :, 0], prm_sb[0:1, 5, g * HG:(g + 1) * HG],
                                ALU.add).then_inc(k_ready, 1)

            dve.wait_ge(mag_done, 1)
            for g in range(NG):
                s = g % 2
                hs = slice(g * HG, (g + 1) * HG)
                t_, g_, c1, c2 = th[:, s], gg[:, g], e1[:, s], e2[:, s]
                pr = small[:, 25, hs].unsqueeze(2).broadcast_to([P, HG, PA])
                pi_ = small[:, 26, hs].unsqueeze(2).broadcast_to([P, HG, PA])
                step(V.scalar_tensor_tensor(out=g_.bitcast(I32), in0=t_.bitcast(I32), scalar=31, in1=g_.bitcast(I32),
                                            op0=ALU.logical_shift_left, op1=ALU.bitwise_xor))
                dve.wait_ge(trig_done, 4 * g + 4)
                w_ = ab[:, s, :, 0:PA]
                step(V.tensor_tensor(w_, c1[:, :, 0:PA], pr, ALU.mult), False)
                step(V.tensor_tensor(c2, c2, pi_, ALU.mult))
                step(V.tensor_tensor(c2, c2, w_, ALU.add))
                V.tensor_tensor(c2, c2, g_[:, :, 0:PA], ALU.mult).then_inc(tab_ready, 1)
                V.tensor_tensor(c1[:, :, PA:], c1[:, :, PA:], g_[:, :, PA:], ALU.mult).then_inc(tab_ready, 1)
                if g + 2 < NG:
                    phases(g + 2)
                if g > 0:
                    taps(g - 1)
            taps(NG - 1)

            def two(v):
                return v.rearrange("p (h n) -> p h n", h=2)

            def mask_input(pair, slot):
                dve.wait_ge(um_in[slot], 4 * (pair - slot) + 16)
                V.tensor_tensor(two(um[:, slot, :]), two(um[:, slot, :]), mask_in, ALU.mult).then_inc(um_ready, 1)

            def mask_output(pair, slot, first):
                dve.wait_ge(conv_ps, pair + 1)
                if not first:
                    dve.wait_ge(x1_ready, pair - 1)
                V.tensor_tensor(two(cv[:, slot, :]), two(ps_c[slot][:, :]), mask_out, ALU.mult).then_inc(conv_sb, 1)

            dve.wait_ge(x_in, 16)
            mask_input(0, 0)
            mask_input(1, 1)
            for pair in range(4):
                mask_input(pair + 2, (pair + 2) % 4)
                mask_output(pair, pair % 2, pair < 2)
            with dve.Fori(1, NH // 8 - 1) as j:
                for i in range(4):
                    mask_input(4 * j + i + 2, (i + 2) % 4)
                    mask_output(4 * j + i, i % 2, False)
            for pair in range(NH // 2 - 4, NH // 2):
                if pair + 2 < NH // 2:
                    mask_input(pair + 2, (pair + 2) % 4)
                mask_output(pair, pair % 2, False)
            dve.wait_ge(amask_ps, 1)
            V.tensor_copy(amask_t[:, :], ps_x[0][:, 0:LR]).then_inc(amaskt_ok, 1)

            def x_lo_part(a, q, first):
                t = 2 * a + q
                dve.wait_ge(xhi_ok, t + 1)
                V.tensor_tensor(x_lo[:, q, :, :], xt[:, :, :], x_hi[:, q, :, :].bitcast(F32),
                                ALU.subtract).then_inc(xlo_ok, 1)

            def b_lo_part(a, q, c, up):
                n = NC * (2 * a + q) + c
                slot, w = (NC * q + c) % 2, CH[c][1]
                dve.wait_ge(b_hi, 2 * n + up + 1)
                V.tensor_tensor(b_spl[LR:P, up, 0:w], b_raw[:, slot, up * w:(up + 1) * w],
                                b_spl[0:LR, up, 0:w].bitcast(F32), ALU.subtract).then_inc(b_lo, 1)

            def td_lo_part(t):
                dve.wait_ge(tdhi_ok, t + 1)
                V.tensor_tensor(td_lo[:, :], ps_x[1][:, 0:P], td_hi[:, :].bitcast(F32), ALU.subtract).then_inc(tdlo_ok, 1)

            def finish(t):
                dve.wait_ge(y_ps, t + 1)
                dve.wait_ge(res_ok, t + 1)
                V.tensor_tensor(y_sb[:, 0:DA_W], y_sb[:, 0:DA_W], ps_da[:, 0:DA_W], ALU.add).then_inc(y_ok, 1)
                V.tensor_tensor(y_sb[:, DA_W:NL], y_sb[:, DA_W:NL], ps_db[:, 0:DB_W], ALU.add).then_inc(y_ok, 1)

            def body(a, q, first, last):
                t = 2 * a + q
                na, nq = (a, 1) if q == 0 else (a + 1, 0)
                dve.wait_ge(a_ps, t + 1)
                wait(dve, tlo_ok, 4 * t)
                V.tensor_tensor(t_m[:, :, :], ps_x[0][:, 0:P].rearrange("p (h b) -> p h b", b=BT), amask[:, :, :],
                                ALU.mult).then_inc(tm_ok, 1)
                dve.wait_ge(thi_ok, 4 * t + 4)
                for up in range(2):
                    rows = slice(up * LR, (up + 1) * LR)
                    src = t_m[rows, :, :].rearrange("p h b -> p (h b)")
                    for half in range(2):
                        V.tensor_tensor(t_lo[half * LR:(half + 1) * LR, up, :], src, t_hi[rows, up, :].bitcast(F32),
                                        ALU.subtract).then_inc(tlo_ok, 1)
                if not first:
                    td_lo_part(t - 1)

                def gated(c):
                    n = NC * t + c
                    s, w = (NC * q + c) % 2, CH[c][1]
                    dve.wait_ge(silu_ok, n + 1)
                    dve.wait_ge(u_ps, n + 1)
                    V.tensor_tensor(h_act[:, s, 0:w], h_act[:, s, 0:w], ps_u[s][:, 0:w], ALU.mult).then_inc(act_ok, 1)

                def ht_lo_part(c):
                    f0, nf = BLK[c]
                    bank = [0, 1, 1][c]
                    dve.wait_ge(hthi_ok, (NC + 1) * t + c + 1 + (c == NC - 1))
                    full = nf if c < NC - 1 else nf - 1
                    V.tensor_tensor(ht_lo[:, f0:f0 + full, :],
                                    ps_x[bank][:, 0:full * P].rearrange("p (f t) -> p f t", t=P),
                                    ht_hi[:, f0:f0 + full, :].bitcast(F32), ALU.subtract).then_inc(htlo_ok, 1)
                    if full < nf:
                        V.tensor_tensor(ht_lo[0:FLAST, f0 + full, :], ps_x[bank][0:FLAST, full * P:nf * P],
                                        ht_hi[0:FLAST, f0 + full, :].bitcast(F32), ALU.subtract).then_inc(htlo_ok, 1)

                dve.wait_ge(ad_hi, t + 1)
                ad = a_raw[:, :, KB * 2 * R:AW].rearrange("p b (f r) -> p f b r", r=R)
                cols = lambda w: w[:, :, NL:NL + LR].rearrange("p f (b r) -> p f b r", r=R)
                V.tensor_tensor(cols(wd_lo), ad, cols(wd_hi).bitcast(F32), ALU.subtract).then_inc(ad_lo, 1)
                b_lo_part(a, q, 1, 0)
                gated(0)
                b_lo_part(a, q, 1, 1)
                if not first:
                    finish(t - 1)
                dve.wait_ge(bd_hi, t + 1)
                V.tensor_tensor(bd_spl[LR:P, :], bd_raw[:, :], bd_spl[0:LR, :].bitcast(F32),
                                ALU.subtract).then_inc(bd_lo, 1)
                b_lo_part(a, q, 2, 0)
                gated(1)
                b_lo_part(a, q, 2, 1)
                ht_lo_part(0)
                if not last:
                    b_lo_part(na, nq, 0, 0)
                gated(2)
                if not last:
                    b_lo_part(na, nq, 0, 1)
                ht_lo_part(1)
                if not last:
                    x_lo_part(na, nq, False)
                ht_lo_part(2)
                dve.wait_ge(down_ps, t + 1)
                wait(dve, td_ps, t)
                both = lambda v: v.unsqueeze(1).broadcast_to([P, 2, LR])
                V.tensor_tensor(td_m[:, :, :], both(ps_db[:, DB_W:DB_W + LR]), both(amask_t[:, :]),
                                ALU.mult).then_inc(td_ok, 1)

            x_lo_part(0, 0, True)
            b_lo_part(0, 0, 0, 0)
            b_lo_part(0, 0, 0, 1)
            dve.wait_ge(amaskt_ok, 1)
            tiles(dve, body)
            td_lo_part(NT - 1)
            finish(NT - 1)

        @block.tensor
        def _(pe):
            T = nc.tensor
            pe.wait_ge(amask_ok, 5)
            pe.wait_ge(ident_s, 2)
            T.transpose(ps_x[0][:, 0:LR], amask[0:LR, :, :].rearrange("p h b -> p (h b)"),
                        ident[0:LR, 0:LR]).then_inc(amask_ps, 1)
            for g in range(NG):
                s = g % 2
                pe.wait_ge(tab_ready, 2 * g + 2)
                if g >= 2:
                    pe.wait_ge(k_ready, g - 1)
                for h in range(HG):
                    last = T.matmul(ps_k[s][0:PA, h * PB:(h + 1) * PB], e2[:, s, h, :], e1[:, s, h, PA:PA + PB],
                                    start=True, stop=True)
                last.then_inc(k_ps, 1)

            def conv(pair, slot, um_slot, first):
                pe.wait_ge(toep_in[slot], 8 * (pair - slot) + 16)
                pe.wait_ge(um_ready, pair + 1)
                if not first:
                    pe.wait_ge(conv_sb, pair - 1)
                for h in range(2):
                    at = h * KB * NB
                    for d in range(KB):
                        n = (KB - d) * NB
                        last = T.matmul(ps_c[slot][:, at + d * NB:at + KB * NB], toep[:, slot, h, d * P:(d + 1) * P],
                                        um[:, um_slot, at:at + n], start=(d == 0), stop=(d == KB - 1))
                last.then_inc(conv_ps, 1)

            for pair in range(4):
                conv(pair, pair % 2, pair, pair < 2)
            with pe.Fori(1, NH // 8) as j:
                for i in range(4):
                    conv(4 * j + i, i % 2, i, False)

            def body(a, q, first, last):
                t = 2 * a + q
                pe.wait_ge(ag_ok, t + 1)
                pe.wait_ge(xt_ok, t + 1)
                wait(pe, res_ok, t)
                if first:
                    pe.wait_ge(amaskt_ok, 1)
                for kb in range(KB):
                    w = a_gu[:, 2 * kb:2 * kb + 2, :, :].rearrange("p g b r -> p (g b r)")
                    ins = T.matmul(ps_x[0][:, 0:P], w, xt[:, kb, :], start=(kb == 0), stop=(kb == KB - 1))
                ins.then_inc(a_ps, 1)

                def base(c, up):
                    n = NC * t + c
                    s, w = (NC * q + c) % 2, CH[c][1]
                    ps = (ps_u if up else ps_g)[s]
                    col = chunk_col(c, up)
                    if c == 0 and not up:
                        pe.wait_ge(xlo_ok, t + 1)
                    if not up:
                        wait(pe, act_ok, n - 1)
                    for kb in range(KB):
                        for xs, ws in ((x_hi, w_hi), (x_hi, w_lo), (x_lo, w_hi)):
                            T.matmul(ps[:, 0:w], xs[:, q, kb, :], ws[:, kb, col:col + w],
                                     start=(kb == 0 and xs is x_hi and ws is w_hi), stop=False)

                def lora(c, up):
                    n = NC * t + c
                    s, w = (NC * q + c) % 2, CH[c][1]
                    ps = (ps_u if up else ps_g)[s]
                    if c == 0 and not up:
                        pe.wait_ge(tlo_ok, 4 * t + 4)
                    pe.wait_ge(b_lo, 2 * n + up + 1)
                    T.matmul(ps[:, 0:w], t_hi[:, up, :], b_spl[:, up, 0:w], start=False, stop=False)
                    T.matmul(ps[:, 0:w], t_lo[:, up, :], b_spl[:, up, 0:w], start=False,
                             stop=True).then_inc(u_ps if up else g_ps, 1)

                def transpose_act(c):
                    f0, nf = BLK[c]
                    s = (NC * q + c) % 2
                    bank = [0, 1, 1][c]
                    pe.wait_ge(act_ok, NC * t + c + 1)
                    if c == 0:
                        pe.wait_ge(tm_ok, t + 1)
                    elif c == 1:
                        wait(pe, tdlo_ok, t)
                    else:
                        pe.wait_ge(htlo_ok, (NC + 1) * t + 2)
                    for f in range(nf):
                        rows = P if f0 + f < FB - 1 else FLAST
                        ins = T.transpose(ps_x[bank][0:rows, f * P:(f + 1) * P], h_act[:, s, f * P:f * P + rows],
                                          ident[:, :])
                    ins.then_inc(ht_ps, 1)

                def down(f0, f1):
                    for f in range(f0, f1):
                        rows = P if f < FB - 1 else FLAST
                        for hs, ws in ((ht_hi, wd_hi), (ht_hi, wd_lo), (ht_lo, wd_hi)):
                            go = f == 0 and hs is ht_hi and ws is wd_hi
                            T.matmul(ps_da[:, 0:DA_W], hs[0:rows, f, :], ws[0:rows, f, 0:DA_W], start=go, stop=False)
                            end = f == FB - 1 and hs is ht_lo
                            ins = T.matmul(ps_db[:, 0:DB_W + LR], hs[0:rows, f, :], ws[0:rows, f, DA_W:NL + LR],
                                           start=go, stop=end)
                    return ins

                base(0, 0)
                if not first:
                    transpose_td(t - 1)
                lora(0, 0)
                base(0, 1)
                lora(0, 1)
                if not first:
                    down_lora(t - 1)
                for up in range(2):
                    base(1, up)
                    lora(1, up)
                transpose_act(0)
                for up in range(2):
                    base(2, up)
                    lora(2, up)
                transpose_act(1)
                pe.wait_ge(htlo_ok, (NC + 1) * t + 1)
                for kb in range(KB):
                    ins = T.transpose(ps_x[0][:, kb * P:(kb + 1) * P], xt[:, kb, :], ident[:, :])
                ins.then_inc(res_ps, 1)
                wait(pe, y_ok, 2 * t)
                pe.wait_ge(ad_lo, t + 1)
                down(*[BLK[0][0], BLK[0][0] + BLK[0][1]])
                transpose_act(2)
                pe.wait_ge(htlo_ok, (NC + 1) * t + 2)
                down(BLK[1][0], BLK[1][0] + BLK[1][1])
                pe.wait_ge(htlo_ok, (NC + 1) * (t + 1))
                down(BLK[2][0], FB).then_inc(down_ps, 1)

            def transpose_td(t):
                pe.wait_ge(td_ok, t + 1)
                pe.wait_ge(htlo_ok, (NC + 1) * (t + 1))
                T.transpose(ps_x[1][:, 0:P], td_m[:, :, :].rearrange("p a r -> p (a r)"), ident[:, :]).then_inc(td_ps, 1)

            def down_lora(t):
                pe.wait_ge(tdlo_ok, t + 1)
                pe.wait_ge(bd_lo, t + 1)
                for ts, end in ((td_hi, False), (td_lo, True)):
                    T.matmul(ps_da[:, 0:DA_W], ts[:, :], bd_spl[:, 0:DA_W], start=False, stop=end)
                    ins = T.matmul(ps_db[:, 0:DB_W], ts[:, :], bd_spl[:, DA_W:NL], start=False, stop=end,
                                   skip_group_check=True)
                ins.then_inc(y_ps, 1)

            pe.wait_ge(stage_lo, len(pieces))
            tiles(pe, body)
            transpose_td(NT - 1)
            down_lora(NT - 1)


def kernel(x, itok_B_8_3872, itok_B_2_6, L0_cond_log_dt, L0_cond_C, L0_cond_log_A_real, L0_cond_A_imag, L0_cond_D,
           L1_cond_W_gate, L1_cond_W_up, L1_cond_W_down, L1_cond_A_gate, L1_cond_B_gate, L1_cond_A_up, L1_cond_B_up,
           L1_cond_A_down, L1_cond_B_down):
    import numpy as np
    import concourse.bacc as bacc
    from concourse.bass_utils import run_bass_kernel_spmd

    xT = np.asarray(x).reshape(NB, NH, KB, P).transpose(3, 1, 2, 0).reshape(P, NH * KB * NB)

    xr = xT.reshape(P, NH // 2, 2 * KB * NB)[::-1].transpose(1, 0, 2).reshape(NH // 2 * P, 2 * KB * NB)

    def interleave(g, u):
        return np.concatenate([m[..., s:s + w] for s, w in CH for m in (g, u)], axis=-1)

    wgu = interleave(np.asarray(L1_cond_W_gate).T, np.asarray(L1_cond_W_up).T)
    wd = np.asarray(L1_cond_W_down).T
    b_gu = interleave(np.asarray(L1_cond_B_gate)[0].transpose(0, 2, 1), np.asarray(L1_cond_B_up)[0].transpose(0, 2, 1))
    b_d = np.asarray(L1_cond_B_down)[0].transpose(0, 2, 1)
    btab = np.concatenate([b_gu, b_d], axis=-1)
    n_ad = btab.shape[0]
    a_g = np.asarray(L1_cond_A_gate)[0].reshape(n_ad, R, KB, P)
    a_u = np.asarray(L1_cond_A_up)[0].reshape(n_ad, R, KB, P)
    a_gu = np.stack([a_g, a_u], axis=1).transpose(0, 4, 3, 1, 2).reshape(n_ad, P, KB * 2 * R)
    a_dn = np.asarray(L1_cond_A_down)[0]
    a_dn = np.concatenate([a_dn, np.zeros((n_ad, R, FB * P - NF), a_dn.dtype)], axis=-1)
    a_dn = a_dn.reshape(n_ad, R, FB, P).transpose(0, 3, 2, 1).reshape(n_ad, P, FB * R)
    atab = np.concatenate([a_gu, a_dn], axis=-1)
    C = np.asarray(L0_cond_C)
    per_mode = [np.asarray(L0_cond_log_A_real).T, np.asarray(L0_cond_A_imag).T, C[..., 0].T, C[..., 1].T]
    rows = [np.broadcast_to(np.asarray(L0_cond_log_dt), (NM, NH))] + per_mode + [
        np.broadcast_to(np.asarray(L0_cond_D), (NM, NH))]
    half = np.concatenate(rows, axis=1)
    prm = np.concatenate([half, half], axis=0)

    arrays = {"xT": xT, "xr": xr, "wgu": wgu, "wd": wd, "atab": atab, "btab": btab, "prm": prm,
              "lens": np.asarray(itok_B_8_3872), "idx": np.asarray(itok_B_2_6)}
    arrays = {k: np.ascontiguousarray(v) for k, v in arrays.items()}
    nc = bacc.Bacc("TRN2", target_bir_lowering=False, num_devices=1, dynamic_dma_scratch_size=1024)
    ins = [nc.dram_tensor(k, v.shape, mybir.dt.from_np(v.dtype), kind="ExternalInput").ap() for k, v in arrays.items()]
    out = nc.dram_tensor("out", (NT * P, NL), F32, kind="ExternalOutput").ap()
    program(nc, *ins, out)
    r = run_bass_kernel_spmd(nc, [arrays], core_ids=[0])
    y = r.results[0]["out"].reshape(NT, NH, BT, NL).transpose(0, 2, 1, 3).reshape(NB, NH, NL)
    return y
```

```python
from contextlib import ExitStack

import concourse.bass as bass
from concourse import mybir

F32 = mybir.dt.float32
F32R = mybir.dt.float32r
I32 = mybir.dt.int32
ALU = mybir.AluOpType
ACT = mybir.ActivationFunctionType

P = 128
NB, NH, NL = 64, 32, 512
KB = NL // P
NM = 64
NF = 1376
FB = -(-NF // P)
FLAST = NF - (FB - 1) * P
R = 16
BT = 4
NT = NB // BT
LR = BT * R
CH = [(0, 512), (512, 512), (1024, NF - 1024)]
NC = len(CH)
BLK = [(0, 4), (4, 4), (8, 3)]
WG = 2 * NF
BW = WG + NL
AW = KB * 2 * R + FB * R
DA_W = 288
DB_W = NL - DA_W
RS = 3
RC = 4
PAIRS = NH // 2
PA, PB = 32, 16
HG = 8
NG = NH // HG
LOG2E, LN2_HI = 1.4426950408889634, 0.693359375
LN2_LO = 0.6931471805599453 - LN2_HI
PI = 3.141592653589793
PI_HI = 3.140625
PI_LO = PI - PI_HI
MAGIC = 12582912.0
ABS_BITS = 0x7FFFFFFF
SCALE = 0.5
N_PRM = 6


def chunk_col(c, up):
    return 2 * CH[c][0] + up * CH[c][1]


def program(nc, xT, xr, wgu, wd, atab, btab, prm, lens, idx, out):
    top = ExitStack()
    with top:
        def sem(name):
            return top.enter_context(nc.semaphore(name))

        def sb(scope, name, shape, dt=F32):
            return scope.enter_context(nc.sbuf_tensor(name, shape, dt))

        kpad = nc.dram_tensor("kpad", (NH, P + NL), F32, kind="Internal")

        w_hi = sb(top, "w_hi", [P, KB, WG], F32R)
        w_lo = sb(top, "w_lo", [P, KB, WG], F32R)
        x = sb(top, "x", [P, NH, KB, NB])
        ident = sb(top, "ident", [P, P])
        amask = sb(top, "amask", [P, NH, BT])
        amask_t = sb(top, "amask_t", [P, LR])
        idx_sb = sb(top, "idx_sb", [1, NB], I32)

        with ExitStack() as pk:
            th = sb(pk, "th", [P, 2, HG, PA + PB])
            rr = sb(pk, "rr", [P, 2, HG, PA + PB])
            ab = sb(pk, "ab", [P, 2, HG, PA + PB])
            e1 = sb(pk, "e1", [P, 2, HG, PA + PB])
            e2 = sb(pk, "e2", [P, 2, HG, PA])
            gg = sb(pk, "gg", [P, NG, HG, PA + PB])
            small = sb(pk, "small", [P, 28, NH])
            prm_sb = sb(pk, "prm_sb", [P, N_PRM, NH])
            lvec = sb(pk, "lvec", [P, PA + PB])
            sgn = sb(pk, "sgn", [P, 1])
            half_pi = sb(pk, "half_pi", [P, 1])
            zeros = sb(pk, "zeros", [NH, P])
            k_sb = sb(pk, "k_sb", [PA, NG, HG, PB])

        wd_hi = sb(top, "wd_hi", [P, FB, NL + LR], F32R)
        wd_lo = sb(top, "wd_lo", [P, FB, NL + LR], F32R)

        with ExitStack() as pa:
            stage = sb(pa, "stage", [P, RS, 2 * 512])
            toep = sb(pa, "toep", [P, RC, 2, NL])
            um = sb(pa, "um", [P, RC, 2 * KB * NB])
            cv = sb(pa, "cv", [P, 2, 2 * KB * NB])
            len_i = sb(pa, "len_i", [P, NB], I32)
            len_f = sb(pa, "len_f", [P, NB])
            lcol = sb(pa, "lcol", [P, 2, KB])
            lmask = sb(pa, "lmask", [P, 2, KB, NB])

        a_gu = sb(top, "a_gu", [P, KB * 2, BT, R])
        a_raw = sb(top, "a_raw", [P, BT, AW])
        b_raw = sb(top, "b_raw", [LR, 2, 2 * 512])
        bd_raw = sb(top, "bd_raw", [LR, NL])
        b_spl = sb(top, "b_spl", [P, 2, 512], F32R)
        bd_spl = sb(top, "bd_spl", [P, NL], F32R)
        xt = sb(top, "xt", [P, KB, P])
        x_hi = sb(top, "x_hi", [P, 2, KB, P], F32R)
        x_lo = sb(top, "x_lo", [P, 2, KB, P], F32R)
        h_act = sb(top, "h_act", [P, 2, 512])
        ht_hi = sb(top, "ht_hi", [P, FB, P], F32R)
        ht_lo = sb(top, "ht_lo", [P, FB, P], F32R)
        y_sb = sb(top, "y_sb", [P, NL])
        t_m = sb(top, "t_m", [P, NH, BT])
        t_hi = sb(top, "t_hi", [P, 2, P], F32R)
        t_lo = sb(top, "t_lo", [P, 2, P], F32R)
        td_m = sb(top, "td_m", [P, 2, LR])
        td_hi = sb(top, "td_hi", [P, P], F32R)
        td_lo = sb(top, "td_lo", [P, P], F32R)

        ps_g = [top.enter_context(nc.psum_tensor(f"ps_g{i}", [P, 512], F32)) for i in range(2)]
        ps_u = [top.enter_context(nc.psum_tensor(f"ps_u{i}", [P, 512], F32)) for i in range(2)]
        ps_da = top.enter_context(nc.psum_tensor("ps_da", [P, 512], F32))
        ps_db = top.enter_context(nc.psum_tensor("ps_db", [P, 512], F32))
        ps_x = [top.enter_context(nc.psum_tensor(f"ps_x{i}", [P, 512], F32)) for i in range(2)]
        ps_k = [ps_da, ps_db]
        ps_c = [ps_g[0], ps_g[1], ps_u[0], ps_u[1]]

        prm_in, len_in, idx_in = sem("prm_in"), sem("len_in"), sem("idx_in")
        x_in = [sem(f"x_in{g}") for g in range(NG)]
        stage_in = [sem(f"stage_in{i}") for i in range(RS)]
        stage_hi, stage_lo = sem("stage_hi"), sem("stage_lo")
        consts, ident_s, amask_ok, amask_ps, amaskt_ok = (sem("consts"), sem("ident_s"), sem("amask_ok"), sem("amask_ps"),
                                                 sem("amaskt_ok"))
        dar_ok = sem("dar_ok")
        steps = sem("steps")
        logmag, mag_done, trig_in, trig_done = sem("logmag"), sem("mag_done"), sem("trig_in"), sem("trig_done")
        ang_in, ang_out, tab_ready = sem("ang_in"), sem("ang_out"), sem("tab_ready")
        k_ps, k_ready, zero_out = sem("k_ps"), sem("k_ready"), sem("zero_out")
        k_out = [sem(f"k_out{g}") for g in range(NG)]
        toep_in = [sem(f"toep_in{i}") for i in range(RC)]
        um_in = [sem(f"um_in{i}") for i in range(RC)]
        um_ready, conv_ps, conv_sb, x1_pool = sem("um_ready"), sem("conv_ps"), sem("conv_sb"), sem("x1_pool")
        x1_dve = sem("x1_dve")
        a_in = sem("a_in")
        ag_ok = sem("ag_ok")
        b_in = [sem("b_in0"), sem("b_in1")]
        bd_in = sem("bd_in")
        b_hi, b_lo = sem("b_hi"), sem("b_lo")
        bd_hi, bd_lo = sem("bd_hi"), sem("bd_lo")
        ad_hi, ad_lo = sem("ad_hi"), sem("ad_lo")
        xt_ok, xhi_ok, xlo_ok = sem("xt_ok"), sem("xhi_ok"), sem("xlo_ok")
        a_ps, tm_ok, thi_ok, tlo_ok = sem("a_ps"), sem("tm_ok"), sem("thi_ok"), sem("tlo_ok")
        g_ps, u_ps, silu_ok, act_ok = sem("g_ps"), sem("u_ps"), sem("silu_ok"), sem("act_ok")
        ht_ps, hthi_ok, htlo_ok = sem("ht_ps"), sem("hthi_ok"), sem("htlo_ok")
        res_ps, res_ok = sem("res_ps"), sem("res_ok")
        down_ps, td_ok, td_ps, tdhi_ok, tdlo_ok = (sem("down_ps"), sem("td_ok"), sem("td_ps"), sem("tdhi_ok"),
                                                   sem("tdlo_ok"))
        y_ps, y_ok, y_out = sem("y_ps"), sem("y_ok"), sem("y_out")

        def wait(eng, s, v):
            if not isinstance(v, int) or v > 0:
                eng.wait_ge(s, v)

        def tiles(eng, body):
            body(0, 0, True, False)
            with eng.Fori(0, NT // 2 - 1) as a:
                body(a, 1, False, False)
                body(a + 1, 0, False, False)
            body(NT // 2 - 1, 1, False, True)

        def chunk_uses(a, q, c):
            return NC * a + (NC * q + c) // 2

        pieces = []
        for kb in range(KB):
            for c in range(NC):
                cols = slice(chunk_col(c, 0), chunk_col(c, 0) + 2 * CH[c][1])
                pieces.append((wgu[kb * P:(kb + 1) * P, cols], w_hi[:, kb, cols], w_lo[:, kb, cols], P, (2 * CH[c][1],)))
        for f0 in range(0, FB - 1, 2):
            pieces.append((wd[f0 * P:(f0 + 2) * P, :].rearrange("(g p) n -> p g n", p=P),
                           wd_hi[:, f0:f0 + 2, 0:NL], wd_lo[:, f0:f0 + 2, 0:NL], P, (2, NL)))
        pieces.append((wd[(FB - 1) * P:NF, :], wd_hi[0:FLAST, FB - 1, 0:NL], wd_lo[0:FLAST, FB - 1, 0:NL], FLAST, (NL,)))

        NP_GU = KB * NC

        def staged(n):
            shape = pieces[n][4]
            size = shape[0] * (shape[1] if len(shape) > 1 else 1)
            v = stage[0:pieces[n][3], n % RS, 0:size]
            return v.rearrange("p (g n) -> p g n", g=2) if len(shape) > 1 else v

        DT, NAR, DAR, DAI = 8, 9, 10, 11

        block = top.enter_context(nc.Block())

        @block.sync
        def _(sp):
            def load_piece(n):
                wait(sp, stage_lo, n - RS + 1)
                sp.dma_start(staged(n), pieces[n][0]).then_inc(stage_in[n % RS], 16)

            def load_x(g):
                hs = slice(g * HG, (g + 1) * HG)
                w = HG * KB * NB
                sp.dma_start(x[:, hs, :, :].rearrange("p h k b -> p (h k b)"),
                             xT[:, g * w:(g + 1) * w]).then_inc(x_in[g], 16)

            def store_taps(g):
                sp.wait_ge(k_ready, g + 1)
                dst = bass.AP(tensor=kpad, offset=g * HG * (P + NL) + P, ap=[[PB, PA], [P + NL, HG], [1, PB]])
                sp.dma_start(dst, k_sb[:, g, :, :]).then_inc(k_out[g], 16)

            def load_toep(pair, slot, group, first):
                sp.wait_ge(k_out[group], 16)
                if not first:
                    sp.wait_ge(conv_ps, pair - RC + 1)
                src = bass.AP(tensor=kpad, offset=pair * (2 * (P + NL)) + 1, ap=[[1, P], [P + NL, 2], [1, NL]])
                sp.dma_start(toep[:, slot, :, :], src).then_inc(toep_in[slot], 16)

            def load_um(pair, slot, first):
                if not first:
                    sp.wait_ge(conv_ps, pair - RC + 1)
                sp.dma_start(um[:, slot, :], xr[bass.ds(pair * P, P), :]).then_inc(um_in[slot], 16)

            sp.dma_start(prm_sb[:, :, :], prm.rearrange("p (a h) -> p a h", a=N_PRM)).then_inc(prm_in, 16)
            load_piece(0)
            load_piece(1)
            sp.dma_start(len_i[:, :], lens.partition_broadcast(P)).then_inc(len_in, 16)
            sp.dma_start(idx_sb[0:1, :], idx.partition_broadcast(1)).then_inc(idx_in, 16)
            sp.wait_ge(consts, 1)
            sp.dma_start(kpad.ap()[:, 0:P], zeros[:, :]).then_inc(zero_out, 16)
            load_piece(2)
            for pair in range(RC):
                load_um(pair, pair, True)
            load_x(0)
            load_piece(3)
            load_x(1)
            load_piece(4)
            load_x(2)
            load_piece(5)
            load_piece(6)
            load_piece(7)
            store_taps(0)
            load_piece(8)
            sp.wait_ge(zero_out, 16)
            for pair in range(RC):
                load_toep(pair, pair, 0, True)
                if pair % 2:
                    load_piece(9 + pair // 2)
            store_taps(1)
            load_piece(11)
            for pair in range(RC, 2 * RC - 1):
                load_toep(pair, pair % RC, 1, False)
                load_um(pair, pair % RC, False)
            store_taps(2)
            load_piece(12)
            load_toep(2 * RC - 1, RC - 1, 1, False)
            load_um(2 * RC - 1, RC - 1, False)
            store_taps(3)
            load_piece(13)
            behind = {8: 14, 9: 15, 10: 16, 11: 17}
            for pair in range(2 * RC, PAIRS):
                load_toep(pair, pair % RC, pair // RC, False)
                load_um(pair, pair % RC, False)
                if pair == 2 * RC + 1:
                    load_x(3)
                if pair in behind:
                    load_piece(behind[pair])

            def indices(a, q):
                return [sp.value_load(idx_sb[0:1, bass.ds((2 * a + q) * BT + b, 1)], min_val=0, max_val=15)
                        for b in range(BT)]

            def load_a(a, q, ids):
                wait(sp, ag_ok, 2 * a + q)
                wait(sp, ad_lo, 2 * a + q)
                for b in range(BT):
                    src = atab[bass.ds(ids[b], 1), :, :].rearrange("a p n -> (a p) n")
                    sp.dma_start(a_raw[:, b, :], src).then_inc(a_in, 16)

            def load_b(a, q, c, ids):
                n = NC * (2 * a + q) + c
                wait(sp, b_lo, 2 * n - 2)
                slot, w = (NC * q + c) % 2, 2 * CH[c][1]
                for b in range(BT):
                    src = btab[bass.ds(ids[b], 1), :, chunk_col(c, 0):chunk_col(c, 0) + w].rearrange("a r n -> (a r) n")
                    sp.dma_start(b_raw[b * R:(b + 1) * R, slot, 0:w], src).then_inc(b_in[slot], 16)

            def load_bd(a, q, ids):
                wait(sp, bd_lo, 2 * a + q)
                for b in range(BT):
                    src = btab[bass.ds(ids[b], 1), :, WG:BW].rearrange("a r n -> (a r) n")
                    sp.dma_start(bd_raw[b * R:(b + 1) * R, :], src).then_inc(bd_in, 16)

            def store(a, q):
                t = 2 * a + q
                sp.wait_ge(y_ok, 2 * t + 2)
                sp.dma_start(out[bass.ds(t * P, P), :], y_sb[:, :]).then_inc(y_out, 16)

            sp.wait_ge(idx_in, 16)
            sp.wait_ge(stage_lo, len(pieces))
            ids0 = indices(0, 0)
            load_a(0, 0, ids0)
            load_b(0, 0, 0, ids0)
            sp.wait_ge(conv_ps, PAIRS - RC + 2)
            load_b(0, 0, 1, ids0)
            load_bd(0, 0, ids0)

            def body(a, q, first, last):
                load_b(a, q, 2, indices(a, q))
                na, nq = (a, 1) if q == 0 else (a + 1, 0)
                if not last:
                    ids = indices(na, nq)
                    load_b(na, nq, 0, ids)
                if not first:
                    store(*((a, 0) if q == 1 else (a - 1, 1)))
                if not last:
                    load_a(na, nq, ids)
                    load_bd(na, nq, ids)
                    load_b(na, nq, 1, ids)

            tiles(sp, body)
            store(NT // 2 - 1, 1)
            sp.wait_ge(y_out, 16 * NT)

        @block.gpsimd
        def _(pool):
            nc.gpsimd.memset(zeros[:, :], 0.0).then_inc(consts, 1)
            nc.gpsimd.iota(lvec[:, 0:PA], pattern=[[PB, PA]], base=0, channel_multiplier=0,
                           allow_small_or_imprecise_dtypes=True).then_inc(consts, 1)
            nc.gpsimd.iota(lvec[:, PA:PA + PB], pattern=[[1, PB]], base=0, channel_multiplier=0,
                           allow_small_or_imprecise_dtypes=True).then_inc(consts, 1)
            for i in range(2):
                nc.gpsimd.iota(lcol[:, i, :], pattern=[[P, KB]], base=(P - 1, 0)[i], channel_multiplier=(-1, 1)[i],
                               allow_small_or_imprecise_dtypes=True).then_inc(consts, 1)
            nc.gpsimd.memset(half_pi[:, :], PI / 2).then_inc(consts, 1)
            nc.gpsimd.memset(ident[:, :], 0.0).then_inc(ident_s, 1)
            pool.wait_ge(ident_s, 1)
            nc.gpsimd.affine_select(out=ident[:, :], in_=ident[:, :], compare_op=ALU.not_equal, fill=1.0, base=0,
                                    pattern=[[-1, P]], channel_multiplier=1).then_inc(ident_s, 1)
            nc.gpsimd.memset(amask[:, :, :], SCALE).then_inc(amask_ok, 1)
            pool.wait_ge(amask_ok, 1)
            for h in range(2):
                v = amask[h * LR:(h + 1) * LR, :, :]
                nc.gpsimd.affine_select(out=v, in_=v, compare_op=ALU.is_ge, fill=0.0, base=0,
                                        pattern=[[0, NH], [-R, BT]], channel_multiplier=1).then_inc(amask_ok, 1)
            pool.wait_ge(amask_ok, 3)
            for h in range(2):
                v = amask[h * LR:(h + 1) * LR, :, :]
                nc.gpsimd.affine_select(out=v, in_=v, compare_op=ALU.is_ge, fill=0.0, base=R - 1,
                                        pattern=[[0, NH], [R, BT]], channel_multiplier=-1).then_inc(amask_ok, 1)
            pool.wait_ge(amask_ok, 5)

            def split_lo(n):
                pool.wait_ge(stage_hi, n + 1)
                nc.gpsimd.tensor_tensor(pieces[n][2], staged(n), pieces[n][1].bitcast(F32),
                                        ALU.subtract).then_inc(stage_lo, 1)

            def add_conv(pair):
                pool.wait_ge(conv_sb, pair + 1)
                v = x[:, 2 * pair:2 * pair + 2, :, :].rearrange("p h k b -> p (h k b)")
                nc.gpsimd.tensor_tensor(v, v, cv[:, pair % 2, :], ALU.add).then_inc(x1_pool, 1)

            split_lo(0)
            pool.wait_ge(consts, 6)
            pool.wait_ge(dar_ok, 1)
            for g in range(NG):
                shape = [P, HG, PA + PB]
                nc.gpsimd.tensor_tensor(gg[:, g], small[:, DAR, g * HG:(g + 1) * HG].unsqueeze(2).broadcast_to(shape),
                                        lvec[:, :].unsqueeze(1).broadcast_to(shape), ALU.mult).then_inc(logmag, 1)
            for n in range(1, NP_GU):
                split_lo(n)
            pool.wait_ge(x_in[0], 16)
            for pair in range(RC):
                add_conv(pair)
            for n in range(NP_GU, len(pieces)):
                split_lo(n)

            def pack_a(t):
                src = a_raw[:, :, 0:KB * 2 * R].rearrange("p b (k r) -> p k b r", r=R)
                nc.gpsimd.tensor_copy(a_gu[:, :, :, :], src).then_inc(ag_ok, 1)

            pool.wait_ge(a_in, 16 * BT)
            pack_a(0)

            def body(a, q, first, last):
                if not last:
                    t = 2 * a + q + 1
                    pool.wait_ge(res_ps, t)
                    pool.wait_ge(xlo_ok, t)
                    pool.wait_ge(a_ps, t)
                    pool.wait_ge(a_in, 16 * BT * (t + 1))
                    pool.wait_ge(x1_dve, PAIRS - RC)
                    nc.gpsimd.tensor_copy(xt[:, :, :].rearrange("p k (h b) -> p k h b", b=BT),
                                          x[:, :, :, bass.ds(t * BT, BT)].rearrange("p h k b -> p k h b")
                                          ).then_inc(xt_ok, 1)
                    pack_a(t)

            tiles(pool, body)

        @block.scalar
        def _(act):
            def split_hi(n):
                act.wait_ge(stage_in[n % RS], 16 * (n // RS + 1))
                nc.scalar.copy(pieces[n][1], staged(n)).then_inc(stage_hi, 1)

            def trig(g):
                s = g % 2
                act.wait_ge(trig_in, g + 1)
                if g >= 2:
                    act.wait_ge(k_ps, g - 1)
                nc.scalar.activation(e1[0:NM, s, :, :], ab[0:NM, s, :, :], ACT.Sin, bias=half_pi[0:NM, :],
                                     scale=-1.0).then_inc(trig_done, 1)
                nc.scalar.activation(e1[NM:P, s, :, :], rr[NM:P, s, :, :], ACT.Sin).then_inc(trig_done, 1)
                nc.scalar.activation(e2[0:NM, s, :, :], rr[0:NM, s, :, 0:PA], ACT.Sin).then_inc(trig_done, 1)
                nc.scalar.activation(e2[NM:P, s, :, :], ab[NM:P, s, :, 0:PA], ACT.Sin, bias=half_pi[NM:P, :],
                                     scale=-1.0).then_inc(trig_done, 1)

            split_hi(0)
            split_hi(1)
            split_hi(2)
            act.wait_ge(consts, 6)
            act.wait_ge(logmag, NG)
            nc.scalar.activation(gg[:, :, :, :], gg[:, :, :, :], ACT.Exp).then_inc(mag_done, 1)
            act.wait_ge(ang_in, 1)
            nc.scalar.activation(small[:, 16, :], small[:, 14, :], ACT.Sin).then_inc(ang_out, 1)
            nc.scalar.activation(small[:, 17, :], small[:, 15, :], ACT.Sin, bias=half_pi[:, :],
                                 scale=-1.0).then_inc(ang_out, 1)
            first_piece = [3, 8, 9, 11, NP_GU]
            for g in range(NG):
                trig(g)
                for n in range(first_piece[g], first_piece[g + 1]):
                    split_hi(n)
            act.wait_ge(k_ready, NG)
            for g in range(NG):
                act.wait_ge(k_out[g], 16)
            for n in range(NP_GU, len(pieces)):
                split_hi(n)

            def x_hi_part(a, q, first):
                t = 2 * a + q
                act.wait_ge(xt_ok, t + 1)
                if first:
                    act.wait_ge(conv_ps, NH // 2)
                    act.wait_ge(stage_lo, len(pieces))
                else:
                    wait(act, u_ps, NC * (t - 1))
                nc.scalar.copy(x_hi[:, q, :, :], xt[:, :, :]).then_inc(xhi_ok, 1)

            def b_hi_part(a, q, c, up):
                n = NC * (2 * a + q) + c
                slot, w = (NC * q + c) % 2, CH[c][1]
                if up == 0:
                    act.wait_ge(b_in[slot], 16 * BT * (chunk_uses(a, q, c) + 1))
                wait(act, u_ps if up else g_ps, n)
                nc.scalar.copy(b_spl[0:LR, up, 0:w], b_raw[:, slot, up * w:(up + 1) * w]).then_inc(b_hi, 1)

            def body(a, q, first, last):
                t = 2 * a + q
                na, nq = (a, 1) if q == 0 else (a + 1, 0)
                act.wait_ge(tm_ok, t + 1)
                wait(act, u_ps, NC * t)
                for up in range(2):
                    src = t_m[up * LR:(up + 1) * LR, :, :].rearrange("p h b -> p (h b)")
                    nc.scalar.copy(t_hi[0:LR, up, :], src).then_inc(thi_ok, 1)
                    nc.scalar.copy(t_hi[LR:P, up, :], src).then_inc(thi_ok, 1)
                if not first:
                    td_hi_part(t - 1)

                def silu(c):
                    n = NC * t + c
                    act.wait_ge(g_ps, n + 1)
                    wait(act, ht_ps, n - 1)
                    s, w = (NC * q + c) % 2, CH[c][1]
                    nc.scalar.activation(h_act[:, s, 0:w], ps_g[s][:, 0:w], ACT.Silu).then_inc(silu_ok, 1)

                def ht_hi_part(c):
                    act.wait_ge(ht_ps, NC * t + c + 1)
                    if c == 0:
                        wait(act, down_ps, t)
                    evacuate(c, ht_hi, c != 0 and 1 or 0)

                def evacuate(c, dst, bank):
                    f0, nf = BLK[c]
                    bank = [0, 1, 1][c]
                    if c < NC - 1:
                        nc.scalar.copy(dst[:, f0:f0 + nf, :],
                                       ps_x[bank][:, 0:nf * P].rearrange("p (f t) -> p f t", t=P)).then_inc(hthi_ok, 1)
                    else:
                        nc.scalar.copy(dst[:, f0:f0 + nf - 1, :],
                                       ps_x[bank][:, 0:(nf - 1) * P].rearrange("p (f t) -> p f t", t=P)).then_inc(hthi_ok, 1)
                        nc.scalar.copy(dst[0:FLAST, f0 + nf - 1, :],
                                       ps_x[bank][0:FLAST, (nf - 1) * P:nf * P]).then_inc(hthi_ok, 1)

                act.wait_ge(a_in, 16 * BT * (t + 1))
                wait(act, down_ps, t)
                ad = a_raw[:, :, KB * 2 * R:AW].rearrange("p b (f r) -> p f b r", r=R)
                nc.scalar.copy(wd_hi[:, :, NL:NL + LR].rearrange("p f (b r) -> p f b r", r=R), ad).then_inc(ad_hi, 1)
                silu(0)
                b_hi_part(a, q, 1, 0)
                b_hi_part(a, q, 1, 1)
                act.wait_ge(bd_in, 16 * BT * (t + 1))
                wait(act, y_ps, t)
                nc.scalar.copy(bd_spl[0:LR, :], bd_raw[:, :]).then_inc(bd_hi, 1)
                silu(1)
                b_hi_part(a, q, 2, 0)
                b_hi_part(a, q, 2, 1)
                ht_hi_part(0)
                silu(2)
                if not last:
                    b_hi_part(na, nq, 0, 0)
                    b_hi_part(na, nq, 0, 1)
                ht_hi_part(1)
                act.wait_ge(res_ps, t + 1)
                wait(act, y_out, 16 * t)
                nc.scalar.copy(y_sb[:, :], ps_x[0][:, :]).then_inc(res_ok, 1)
                if not last:
                    x_hi_part(na, nq, False)
                ht_hi_part(2)

            def td_hi_part(t):
                act.wait_ge(td_ps, t + 1)
                wait(act, y_ps, t)
                nc.scalar.copy(td_hi[:, :], ps_x[1][:, 0:P]).then_inc(tdhi_ok, 1)

            x_hi_part(0, 0, True)
            b_hi_part(0, 0, 0, 0)
            b_hi_part(0, 0, 0, 1)
            tiles(act, body)
            td_hi_part(NT - 1)

        @block.vector
        def _(dve):
            count = [0]

            def step(ins, now=True):
                count[0] += 1
                ins.then_inc(steps, 1)
                if now:
                    dve.wait_ge(steps, count[0])

            def sm(i, n=1):
                return small[:, i:i + n, :]

            V = nc.vector

            def exp_parts(src, at, n):
                q_, s_, r_, k_ = sm(at, n), sm(at + n, n), sm(at + 2 * n, n), sm(at + 3 * n, n)
                step(V.tensor_scalar(r_, src, 88.0, -87.0, ALU.min, ALU.max))
                step(V.tensor_scalar(s_, r_, LOG2E, MAGIC + 127.0, ALU.mult, ALU.add))
                step(V.tensor_scalar(k_, s_, MAGIC + 127.0, None, ALU.subtract))
                step(V.tensor_scalar(s_.bitcast(I32), s_.bitcast(I32), 23, None, ALU.logical_shift_left))
                step(V.scalar_tensor_tensor(out=r_, in0=k_, scalar=-LN2_HI, in1=r_, op0=ALU.mult, op1=ALU.add))
                step(V.scalar_tensor_tensor(out=r_, in0=k_, scalar=-LN2_LO, in1=r_, op0=ALU.mult, op1=ALU.add))
                step(V.tensor_scalar(q_, r_, 1 / 5040, None, ALU.mult))
                for c in (1 / 720, 1 / 120, 1 / 24, 1 / 6, 1 / 2, 1.0):
                    step(V.scalar_tensor_tensor(out=q_, in0=q_, scalar=c, in1=r_, op0=ALU.add, op1=ALU.mult))
                return q_, s_

            def stt(o, i, i0, s, i1, op0, op1):
                step(V.scalar_tensor_tensor(out=sm(o), in0=sm(i0), scalar=s, in1=i1, op0=op0, op1=op1))

            step(V.memset(sgn[0:NM, :], 1.0), False)
            step(V.memset(sgn[NM:P, :], -1.0), False)
            prm_ = lambda i, n=1: prm_sb[:, i:i + n, :]
            dve.wait_ge(prm_in, 16)
            q_, s_ = exp_parts(prm_(0, 2), 0, 2)
            step(V.scalar_tensor_tensor(out=sm(8, 2), in0=q_, scalar=1.0, in1=s_, op0=ALU.add, op1=ALU.mult))
            V.scalar_tensor_tensor(out=sm(DAR), in0=sm(NAR), scalar=-1.0, in1=sm(DT), op0=ALU.mult,
                                   op1=ALU.mult).then_inc(dar_ok, 1)
            step(V.tensor_tensor(sm(DAI), prm_(2), sm(DT), ALU.mult))
            dve.wait_ge(consts, 6)
            step(V.tensor_scalar(sm(12), sm(DAI), 0.5, None, ALU.mult))
            step(V.tensor_scalar(sm(13), sm(12), 1 / PI, MAGIC, ALU.mult, ALU.add))
            step(V.tensor_scalar(sm(13), sm(13), MAGIC, None, ALU.subtract))
            step(V.scalar_tensor_tensor(out=sm(14), in0=sm(13), scalar=-PI_HI, in1=sm(12), op0=ALU.mult, op1=ALU.add))
            step(V.scalar_tensor_tensor(out=sm(14), in0=sm(13), scalar=-PI_LO, in1=sm(14), op0=ALU.mult, op1=ALU.add))
            V.tensor_scalar(sm(15).bitcast(I32), sm(14).bitcast(I32), ABS_BITS, None, ALU.bitwise_and).then_inc(ang_in, 1)

            def phases(g):
                s = g % 2
                hs = slice(g * HG, (g + 1) * HG)
                shape = [P, HG, PA + PB]
                lv = lvec[:, :].unsqueeze(1).broadcast_to(shape)
                dai = small[:, DAI, hs].unsqueeze(2).broadcast_to(shape)
                t_, r_, a_ = th[:, s], rr[:, s], ab[:, s]
                step(V.tensor_tensor(r_, dai, lv, ALU.mult))
                step(V.tensor_scalar(t_, r_, 1 / PI, MAGIC, ALU.mult, ALU.add))
                step(V.tensor_scalar(a_, t_, MAGIC, None, ALU.subtract))
                step(V.scalar_tensor_tensor(out=r_, in0=a_, scalar=-PI_HI, in1=r_, op0=ALU.mult, op1=ALU.add))
                step(V.scalar_tensor_tensor(out=r_, in0=a_, scalar=-PI_LO, in1=r_, op0=ALU.mult, op1=ALU.add))
                V.tensor_scalar(a_.bitcast(I32), r_.bitcast(I32), ABS_BITS, None, ALU.bitwise_and).then_inc(trig_in, 1)

            phases(0)
            dve.wait_ge(dar_ok, 1)
            q_, s_ = exp_parts(sm(DAR), 0, 1)
            step(V.tensor_tensor(sm(4), q_, s_, ALU.mult))
            step(V.scalar_tensor_tensor(out=sm(4), in0=s_, scalar=-1.0, in1=sm(4), op0=ALU.add, op1=ALU.add))
            dve.wait_ge(ang_out, 2)
            SI, CO, EM = 16, 17, 4
            step(V.tensor_tensor(sm(19), sm(SI), sm(SI), ALU.mult))
            step(V.tensor_scalar(sm(20), sm(19), -2.0, 1.0, ALU.mult, ALU.add))
            step(V.tensor_tensor(sm(20), sm(20), sm(EM), ALU.mult))
            step(V.scalar_tensor_tensor(out=sm(20), in0=sm(19), scalar=-2.0, in1=sm(20), op0=ALU.mult, op1=ALU.add))
            step(V.tensor_tensor(sm(21), sm(SI), sm(CO), ALU.mult))
            step(V.tensor_scalar(sm(21), sm(21), 2.0, None, ALU.mult))
            step(V.scalar_tensor_tensor(out=sm(21), in0=sm(EM), scalar=1.0, in1=sm(21), op0=ALU.add, op1=ALU.mult))
            XR, YI = 20, 21
            step(V.tensor_tensor(sm(22), sm(NAR), sm(NAR), ALU.mult), False)
            step(V.tensor_tensor(sm(23), prm_(2), prm_(2), ALU.mult))
            step(V.tensor_tensor(sm(22), sm(22), sm(23), ALU.add))
            step(V.reciprocal(sm(22), sm(22)))
            step(V.tensor_tensor(sm(23), sm(YI), prm_(2), ALU.mult), False)
            step(V.tensor_tensor(sm(24), sm(XR), sm(NAR), ALU.mult))
            step(V.tensor_tensor(sm(23), sm(23), sm(24), ALU.subtract))
            step(V.tensor_tensor(sm(23), sm(23), sm(22), ALU.mult), False)
            step(V.tensor_tensor(sm(24), sm(XR), prm_(2), ALU.mult), False)
            step(V.tensor_tensor(sm(25), sm(YI), sm(NAR), ALU.mult))
            step(V.scalar_tensor_tensor(out=sm(24), in0=sm(24), scalar=-1.0, in1=sm(25), op0=ALU.mult, op1=ALU.subtract))
            step(V.tensor_tensor(sm(24), sm(24), sm(22), ALU.mult))
            step(V.tensor_tensor(sm(25), prm_(3), sm(23), ALU.mult), False)
            step(V.tensor_tensor(sm(26), prm_(4), sm(24), ALU.mult))
            step(V.tensor_tensor(sm(25), sm(25), sm(26), ALU.subtract))
            step(V.tensor_tensor(sm(26), prm_(3), sm(24), ALU.mult), False)
            step(V.tensor_tensor(sm(27), prm_(4), sm(23), ALU.mult))
            step(V.tensor_tensor(sm(26), sm(26), sm(27), ALU.add))
            step(V.tensor_scalar(sm(25), sm(25), sgn[:, :], 2.0, ALU.mult, ALU.mult))
            step(V.tensor_scalar(sm(26), sm(26), -2.0, None, ALU.mult))

            def taps(g):
                dve.wait_ge(k_ps, g + 1)
                step(V.tensor_copy(k_sb[:, g, :, :], ps_k[g % 2][0:PA, 0:HG * PB].rearrange("a (h b) -> a h b", b=PB)))
                V.tensor_tensor(k_sb[0:1, g, :, 0], k_sb[0:1, g, :, 0], prm_sb[0:1, 5, g * HG:(g + 1) * HG],
                                ALU.add).then_inc(k_ready, 1)

            def tables(g):
                s = g % 2
                hs = slice(g * HG, (g + 1) * HG)
                t_, g_, c1, c2 = th[:, s], gg[:, g], e1[:, s], e2[:, s]
                pr = small[:, 25, hs].unsqueeze(2).broadcast_to([P, HG, PA])
                pi_ = small[:, 26, hs].unsqueeze(2).broadcast_to([P, HG, PA])
                step(V.scalar_tensor_tensor(out=g_.bitcast(I32), in0=t_.bitcast(I32), scalar=31, in1=g_.bitcast(I32),
                                            op0=ALU.logical_shift_left, op1=ALU.bitwise_xor))
                dve.wait_ge(trig_done, 4 * g + 4)
                w_ = ab[:, s, :, 0:PA]
                step(V.tensor_tensor(w_, c1[:, :, 0:PA], pr, ALU.mult), False)
                step(V.tensor_tensor(c2, c2, pi_, ALU.mult))
                step(V.tensor_tensor(c2, c2, w_, ALU.add))
                V.tensor_tensor(c2, c2, g_[:, :, 0:PA], ALU.mult).then_inc(tab_ready, 1)
                V.tensor_tensor(c1[:, :, PA:], c1[:, :, PA:], g_[:, :, PA:], ALU.mult).then_inc(tab_ready, 1)

            def two(v):
                return v.rearrange("p (h n) -> p h n", h=2)

            def mask_input(pair, slot):
                dve.wait_ge(um_in[slot], 4 * (pair - slot) + 16)
                V.tensor_tensor(two(um[:, slot, :]), two(um[:, slot, :]), mask_in, ALU.mult).then_inc(um_ready, 1)

            def mask_output(pair, slot):
                dve.wait_ge(conv_ps, pair + 1)
                V.tensor_tensor(two(cv[:, slot % 2, :]), two(ps_c[slot][:, :]), mask_out, ALU.mult).then_inc(conv_sb, 1)

            def add_conv(pair, slot):
                v = x[:, bass.ds(2 * pair, 2), :, :].rearrange("p h k b -> p (h k b)")
                dve.wait_ge(conv_sb, pair + 1)
                V.tensor_tensor(v, v, cv[:, slot % 2, :], ALU.add).then_inc(x1_dve, 1)

            dve.wait_ge(mag_done, 1)
            tables(0)
            dve.wait_ge(len_in, 16)
            step(V.tensor_copy(len_f[:, :], len_i[:, :]))
            for i in range(2):
                for kb in range(KB):
                    step(V.tensor_scalar(lmask[:, i, kb, :], len_f[:, :], lcol[:, i, kb:kb + 1], None, ALU.is_gt), False)
            dve.wait_ge(steps, count[0])
            mask_in, mask_out = (lmask[:, i, :, :].rearrange("p k b -> p (k b)").unsqueeze(1).broadcast_to([P, 2, KB * NB])
                                 for i in range(2))

            taps(0)
            phases(1)
            mask_input(0, 0)
            mask_input(1, 1)
            phases(2)
            tables(1)
            mask_input(2, 2)
            mask_input(3, 3)
            taps(1)
            phases(3)
            tables(2)
            mask_output(0, 0)
            mask_input(4, 0)
            taps(2)
            tables(3)
            mask_output(1, 1)
            taps(3)
            mask_input(5, 1)
            for pair in (2, 3):
                dve.wait_ge(x1_pool, pair - 1)
                mask_output(pair, pair)
            mask_input(6, 2)
            dve.wait_ge(x1_pool, RC)
            for g in range(1, NG - 1):
                dve.wait_ge(x_in[g], 16)
            with dve.Fori(1, NG - 1) as j:
                for i in range(RC):
                    mask_output(RC * j + i, i)
                    mask_input(RC * j + i + 3, (i + 3) % RC)
                    add_conv(RC * j + i, i)
            dve.wait_ge(x_in[NG - 1], 16)
            for pair in range(PAIRS - RC, PAIRS):
                mask_output(pair, pair % RC)
                if pair + 3 < PAIRS:
                    mask_input(pair + 3, (pair + 3) % RC)
                add_conv(pair, pair % RC)
            dve.wait_ge(x1_dve, PAIRS - RC)
            V.tensor_copy(xt[:, :, :].rearrange("p k (h b) -> p k h b", b=BT),
                          x[:, :, :, 0:BT].rearrange("p h k b -> p k h b")).then_inc(xt_ok, 1)
            dve.wait_ge(amask_ps, 1)
            V.tensor_copy(amask_t[:, :], ps_x[0][:, 0:LR]).then_inc(amaskt_ok, 1)

            def x_lo_part(a, q, first):
                t = 2 * a + q
                dve.wait_ge(xhi_ok, t + 1)
                V.tensor_tensor(x_lo[:, q, :, :], xt[:, :, :], x_hi[:, q, :, :].bitcast(F32),
                                ALU.subtract).then_inc(xlo_ok, 1)

            def b_lo_part(a, q, c, up):
                n = NC * (2 * a + q) + c
                slot, w = (NC * q + c) % 2, CH[c][1]
                dve.wait_ge(b_hi, 2 * n + up + 1)
                V.tensor_tensor(b_spl[LR:P, up, 0:w], b_raw[:, slot, up * w:(up + 1) * w],
                                b_spl[0:LR, up, 0:w].bitcast(F32), ALU.subtract).then_inc(b_lo, 1)

            def td_lo_part(t):
                dve.wait_ge(tdhi_ok, t + 1)
                V.tensor_tensor(td_lo[:, :], ps_x[1][:, 0:P], td_hi[:, :].bitcast(F32), ALU.subtract).then_inc(tdlo_ok, 1)

            def finish(t):
                dve.wait_ge(y_ps, t + 1)
                dve.wait_ge(res_ok, t + 1)
                V.tensor_tensor(y_sb[:, 0:DA_W], y_sb[:, 0:DA_W], ps_da[:, 0:DA_W], ALU.add).then_inc(y_ok, 1)
                V.tensor_tensor(y_sb[:, DA_W:NL], y_sb[:, DA_W:NL], ps_db[:, 0:DB_W], ALU.add).then_inc(y_ok, 1)

            def body(a, q, first, last):
                t = 2 * a + q
                na, nq = (a, 1) if q == 0 else (a + 1, 0)
                dve.wait_ge(a_ps, t + 1)
                wait(dve, tlo_ok, 4 * t)
                V.tensor_tensor(t_m[:, :, :], ps_x[0][:, 0:P].rearrange("p (h b) -> p h b", b=BT), amask[:, :, :],
                                ALU.mult).then_inc(tm_ok, 1)
                dve.wait_ge(thi_ok, 4 * t + 4)
                for up in range(2):
                    rows = slice(up * LR, (up + 1) * LR)
                    src = t_m[rows, :, :].rearrange("p h b -> p (h b)")
                    for half in range(2):
                        V.tensor_tensor(t_lo[half * LR:(half + 1) * LR, up, :], src, t_hi[rows, up, :].bitcast(F32),
                                        ALU.subtract).then_inc(tlo_ok, 1)
                if not first:
                    td_lo_part(t - 1)

                def gated(c):
                    n = NC * t + c
                    s, w = (NC * q + c) % 2, CH[c][1]
                    dve.wait_ge(silu_ok, n + 1)
                    dve.wait_ge(u_ps, n + 1)
                    V.tensor_tensor(h_act[:, s, 0:w], h_act[:, s, 0:w], ps_u[s][:, 0:w], ALU.mult).then_inc(act_ok, 1)

                def ht_lo_part(c):
                    f0, nf = BLK[c]
                    bank = [0, 1, 1][c]
                    dve.wait_ge(hthi_ok, (NC + 1) * t + c + 1 + (c == NC - 1))
                    full = nf if c < NC - 1 else nf - 1
                    V.tensor_tensor(ht_lo[:, f0:f0 + full, :],
                                    ps_x[bank][:, 0:full * P].rearrange("p (f t) -> p f t", t=P),
                                    ht_hi[:, f0:f0 + full, :].bitcast(F32), ALU.subtract).then_inc(htlo_ok, 1)
                    if full < nf:
                        V.tensor_tensor(ht_lo[0:FLAST, f0 + full, :], ps_x[bank][0:FLAST, full * P:nf * P],
                                        ht_hi[0:FLAST, f0 + full, :].bitcast(F32), ALU.subtract).then_inc(htlo_ok, 1)

                dve.wait_ge(ad_hi, t + 1)
                ad = a_raw[:, :, KB * 2 * R:AW].rearrange("p b (f r) -> p f b r", r=R)
                cols = lambda w: w[:, :, NL:NL + LR].rearrange("p f (b r) -> p f b r", r=R)
                V.tensor_tensor(cols(wd_lo), ad, cols(wd_hi).bitcast(F32), ALU.subtract).then_inc(ad_lo, 1)
                b_lo_part(a, q, 1, 0)
                gated(0)
                b_lo_part(a, q, 1, 1)
                if not first:
                    finish(t - 1)
                dve.wait_ge(bd_hi, t + 1)
                V.tensor_tensor(bd_spl[LR:P, :], bd_raw[:, :], bd_spl[0:LR, :].bitcast(F32),
                                ALU.subtract).then_inc(bd_lo, 1)
                b_lo_part(a, q, 2, 0)
                gated(1)
                b_lo_part(a, q, 2, 1)
                ht_lo_part(0)
                if not last:
                    b_lo_part(na, nq, 0, 0)
                gated(2)
                if not last:
                    b_lo_part(na, nq, 0, 1)
                ht_lo_part(1)
                if not last:
                    x_lo_part(na, nq, False)
                ht_lo_part(2)
                dve.wait_ge(down_ps, t + 1)
                wait(dve, td_ps, t)
                both = lambda v: v.unsqueeze(1).broadcast_to([P, 2, LR])
                V.tensor_tensor(td_m[:, :, :], both(ps_db[:, DB_W:DB_W + LR]), both(amask_t[:, :]),
                                ALU.mult).then_inc(td_ok, 1)

            x_lo_part(0, 0, True)
            b_lo_part(0, 0, 0, 0)
            b_lo_part(0, 0, 0, 1)
            dve.wait_ge(amaskt_ok, 1)
            tiles(dve, body)
            td_lo_part(NT - 1)
            finish(NT - 1)

        @block.tensor
        def _(pe):
            T = nc.tensor
            def taps(g):
                s = g % 2
                pe.wait_ge(tab_ready, 2 * g + 2)
                if g >= 2:
                    pe.wait_ge(k_ready, g - 1)
                for h in range(HG):
                    last = T.matmul(ps_k[s][0:PA, h * PB:(h + 1) * PB], e2[:, s, h, :], e1[:, s, h, PA:PA + PB],
                                    start=True, stop=True)
                last.then_inc(k_ps, 1)

            def conv(pair, slot, first):
                pe.wait_ge(toep_in[slot], 4 * (pair - slot) + 16)
                pe.wait_ge(um_ready, pair + 1)
                if not first:
                    pe.wait_ge(conv_sb, pair - RC + 1)
                for h in range(2):
                    at = h * KB * NB
                    for d in range(KB):
                        n = (KB - d) * NB
                        last = T.matmul(ps_c[slot][:, at + d * NB:at + KB * NB], toep[:, slot, h, d * P:(d + 1) * P],
                                        um[:, slot, at:at + n], start=(d == 0), stop=(d == KB - 1))
                last.then_inc(conv_ps, 1)

            taps(0)
            conv(0, 0, True)
            taps(1)
            conv(1, 1, True)
            conv(2, 2, True)
            taps(2)
            conv(3, 3, True)
            taps(3)
            conv(4, 0, False)
            with pe.Fori(1, NG - 1) as j:
                for i in range(1, RC + 1):
                    conv(RC * j + i, i % RC, False)
            for pair in range(PAIRS - RC + 1, PAIRS):
                conv(pair, pair % RC, False)
            pe.wait_ge(amask_ok, 5)
            pe.wait_ge(ident_s, 2)
            T.transpose(ps_x[0][:, 0:LR], amask[0:LR, :, :].rearrange("p h b -> p (h b)"),
                        ident[0:LR, 0:LR]).then_inc(amask_ps, 1)
            def body(a, q, first, last):
                t = 2 * a + q
                pe.wait_ge(ag_ok, t + 1)
                pe.wait_ge(xt_ok, t + 1)
                wait(pe, res_ok, t)
                if first:
                    pe.wait_ge(amaskt_ok, 1)
                for kb in range(KB):
                    w = a_gu[:, 2 * kb:2 * kb + 2, :, :].rearrange("p g b r -> p (g b r)")
                    ins = T.matmul(ps_x[0][:, 0:P], w, xt[:, kb, :], start=(kb == 0), stop=(kb == KB - 1))
                ins.then_inc(a_ps, 1)

                def base(c, up):
                    n = NC * t + c
                    s, w = (NC * q + c) % 2, CH[c][1]
                    ps = (ps_u if up else ps_g)[s]
                    col = chunk_col(c, up)
                    if c == 0 and not up:
                        pe.wait_ge(xlo_ok, t + 1)
                    if not up:
                        wait(pe, act_ok, n - 1)
                    for kb in range(KB):
                        for xs, ws in ((x_hi, w_hi), (x_hi, w_lo), (x_lo, w_hi)):
                            T.matmul(ps[:, 0:w], xs[:, q, kb, :], ws[:, kb, col:col + w],
                                     start=(kb == 0 and xs is x_hi and ws is w_hi), stop=False)

                def lora(c, up):
                    n = NC * t + c
                    s, w = (NC * q + c) % 2, CH[c][1]
                    ps = (ps_u if up else ps_g)[s]
                    if c == 0 and not up:
                        pe.wait_ge(tlo_ok, 4 * t + 4)
                    pe.wait_ge(b_lo, 2 * n + up + 1)
                    T.matmul(ps[:, 0:w], t_hi[:, up, :], b_spl[:, up, 0:w], start=False, stop=False)
                    T.matmul(ps[:, 0:w], t_lo[:, up, :], b_spl[:, up, 0:w], start=False,
                             stop=True).then_inc(u_ps if up else g_ps, 1)

                def transpose_act(c):
                    f0, nf = BLK[c]
                    s = (NC * q + c) % 2
                    bank = [0, 1, 1][c]
                    pe.wait_ge(act_ok, NC * t + c + 1)
                    if c == 0:
                        pe.wait_ge(tm_ok, t + 1)
                    elif c == 1:
                        wait(pe, tdlo_ok, t)
                    else:
                        pe.wait_ge(htlo_ok, (NC + 1) * t + 2)
                    for f in range(nf):
                        rows = P if f0 + f < FB - 1 else FLAST
                        ins = T.transpose(ps_x[bank][0:rows, f * P:(f + 1) * P], h_act[:, s, f * P:f * P + rows],
                                          ident[:, :])
                    ins.then_inc(ht_ps, 1)

                def down(f0, f1):
                    for f in range(f0, f1):
                        rows = P if f < FB - 1 else FLAST
                        for hs, ws in ((ht_hi, wd_hi), (ht_hi, wd_lo), (ht_lo, wd_hi)):
                            go = f == 0 and hs is ht_hi and ws is wd_hi
                            T.matmul(ps_da[:, 0:DA_W], hs[0:rows, f, :], ws[0:rows, f, 0:DA_W], start=go, stop=False)
                            end = f == FB - 1 and hs is ht_lo
                            ins = T.matmul(ps_db[:, 0:DB_W + LR], hs[0:rows, f, :], ws[0:rows, f, DA_W:NL + LR],
                                           start=go, stop=end)
                    return ins

                base(0, 0)
                if not first:
                    transpose_td(t - 1)
                lora(0, 0)
                base(0, 1)
                lora(0, 1)
                if not first:
                    down_lora(t - 1)
                for up in range(2):
                    base(1, up)
                    lora(1, up)
                transpose_act(0)
                for up in range(2):
                    base(2, up)
                    lora(2, up)
                transpose_act(1)
                pe.wait_ge(htlo_ok, (NC + 1) * t + 1)
                for kb in range(KB):
                    ins = T.transpose(ps_x[0][:, kb * P:(kb + 1) * P], xt[:, kb, :], ident[:, :])
                ins.then_inc(res_ps, 1)
                wait(pe, y_ok, 2 * t)
                pe.wait_ge(ad_lo, t + 1)
                down(*[BLK[0][0], BLK[0][0] + BLK[0][1]])
                transpose_act(2)
                pe.wait_ge(htlo_ok, (NC + 1) * t + 2)
                down(BLK[1][0], BLK[1][0] + BLK[1][1])
                pe.wait_ge(htlo_ok, (NC + 1) * (t + 1))
                down(BLK[2][0], FB).then_inc(down_ps, 1)

            def transpose_td(t):
                pe.wait_ge(td_ok, t + 1)
                pe.wait_ge(htlo_ok, (NC + 1) * (t + 1))
                T.transpose(ps_x[1][:, 0:P], td_m[:, :, :].rearrange("p a r -> p (a r)"), ident[:, :]).then_inc(td_ps, 1)

            def down_lora(t):
                pe.wait_ge(tdlo_ok, t + 1)
                pe.wait_ge(bd_lo, t + 1)
                for ts, end in ((td_hi, False), (td_lo, True)):
                    T.matmul(ps_da[:, 0:DA_W], ts[:, :], bd_spl[:, 0:DA_W], start=False, stop=end)
                    ins = T.matmul(ps_db[:, 0:DB_W], ts[:, :], bd_spl[:, DA_W:NL], start=False, stop=end,
                                   skip_group_check=True)
                ins.then_inc(y_ps, 1)

            pe.wait_ge(stage_lo, len(pieces))
            tiles(pe, body)
            transpose_td(NT - 1)
            down_lora(NT - 1)


def kernel(x, itok_B_8_3872, itok_B_2_6, L0_cond_log_dt, L0_cond_C, L0_cond_log_A_real, L0_cond_A_imag, L0_cond_D,
           L1_cond_W_gate, L1_cond_W_up, L1_cond_W_down, L1_cond_A_gate, L1_cond_B_gate, L1_cond_A_up, L1_cond_B_up,
           L1_cond_A_down, L1_cond_B_down):
    import numpy as np
    import concourse.bacc as bacc
    from concourse.bass_utils import run_bass_kernel_spmd

    xT = np.asarray(x).reshape(NB, NH, KB, P).transpose(3, 1, 2, 0).reshape(P, NH * KB * NB)

    xr = xT.reshape(P, NH // 2, 2 * KB * NB)[::-1].transpose(1, 0, 2).reshape(NH // 2 * P, 2 * KB * NB)

    def interleave(g, u):
        return np.concatenate([m[..., s:s + w] for s, w in CH for m in (g, u)], axis=-1)

    wgu = interleave(np.asarray(L1_cond_W_gate).T, np.asarray(L1_cond_W_up).T)
    wd = np.asarray(L1_cond_W_down).T
    b_gu = interleave(np.asarray(L1_cond_B_gate)[0].transpose(0, 2, 1), np.asarray(L1_cond_B_up)[0].transpose(0, 2, 1))
    b_d = np.asarray(L1_cond_B_down)[0].transpose(0, 2, 1)
    btab = np.concatenate([b_gu, b_d], axis=-1)
    n_ad = btab.shape[0]
    a_g = np.asarray(L1_cond_A_gate)[0].reshape(n_ad, R, KB, P)
    a_u = np.asarray(L1_cond_A_up)[0].reshape(n_ad, R, KB, P)
    a_gu = np.stack([a_g, a_u], axis=1).transpose(0, 4, 3, 1, 2).reshape(n_ad, P, KB * 2 * R)
    a_dn = np.asarray(L1_cond_A_down)[0]
    a_dn = np.concatenate([a_dn, np.zeros((n_ad, R, FB * P - NF), a_dn.dtype)], axis=-1)
    a_dn = a_dn.reshape(n_ad, R, FB, P).transpose(0, 3, 2, 1).reshape(n_ad, P, FB * R)
    atab = np.concatenate([a_gu, a_dn], axis=-1)
    C = np.asarray(L0_cond_C)
    per_mode = [np.asarray(L0_cond_log_A_real).T, np.asarray(L0_cond_A_imag).T, C[..., 0].T, C[..., 1].T]
    rows = [np.broadcast_to(np.asarray(L0_cond_log_dt), (NM, NH))] + per_mode + [
        np.broadcast_to(np.asarray(L0_cond_D), (NM, NH))]
    half = np.concatenate(rows, axis=1)
    prm = np.concatenate([half, half], axis=0)

    arrays = {"xT": xT, "xr": xr, "wgu": wgu, "wd": wd, "atab": atab, "btab": btab, "prm": prm,
              "lens": np.asarray(itok_B_8_3872), "idx": np.asarray(itok_B_2_6)}
    arrays = {k: np.ascontiguousarray(v) for k, v in arrays.items()}
    nc = bacc.Bacc("TRN2", target_bir_lowering=False, num_devices=1, dynamic_dma_scratch_size=1024)
    ins = [nc.dram_tensor(k, v.shape, mybir.dt.from_np(v.dtype), kind="ExternalInput").ap() for k, v in arrays.items()]
    out = nc.dram_tensor("out", (NT * P, NL), F32, kind="ExternalOutput").ap()
    program(nc, *ins, out)
    r = run_bass_kernel_spmd(nc, [arrays], core_ids=[0])
    y = r.results[0]["out"].reshape(NT, NH, BT, NL).transpose(0, 2, 1, 3).reshape(NB, NH, NL)
    return y
```

```python
from contextlib import ExitStack

import concourse.bass as bass
from concourse import mybir

F32 = mybir.dt.float32
F32R = mybir.dt.float32r
I32 = mybir.dt.int32
ALU = mybir.AluOpType
ACT = mybir.ActivationFunctionType

P = 128
NB, NH, NL = 64, 32, 512
KB = NL // P
NM = 64
NF = 1376
FB = -(-NF // P)
FLAST = NF - (FB - 1) * P
R = 16
BT = 4
NT = NB // BT
LR = BT * R
CH = [(0, 512), (512, 512), (1024, NF - 1024)]
NC = len(CH)
BLK = [(0, 4), (4, 4), (8, 3)]
WG = 2 * NF
BW = WG + NL
AW = KB * 2 * R + FB * R
DA_W = 288
DB_W = NL - DA_W
RS = 3
RC = 4
PAIRS = NH // 2
PA, PB = 32, 16
HG = 8
NG = NH // HG
LOG2E, LN2_HI = 1.4426950408889634, 0.693359375
LN2_LO = 0.6931471805599453 - LN2_HI
PI = 3.141592653589793
PI_HI = 3.140625
PI_LO = PI - PI_HI
MAGIC = 12582912.0
ABS_BITS = 0x7FFFFFFF
SCALE = 0.5
N_PRM = 6


def chunk_col(c, up):
    return 2 * CH[c][0] + up * CH[c][1]


def program(nc, xT, xr, wgu, wd, atab, btab, prm, lens, idx, out):
    top = ExitStack()
    with top:
        def sem(name):
            return top.enter_context(nc.semaphore(name))

        def sb(scope, name, shape, dt=F32):
            return scope.enter_context(nc.sbuf_tensor(name, shape, dt))

        kpad = nc.dram_tensor("kpad", (NH, P + NL), F32, kind="Internal")

        w_hi = sb(top, "w_hi", [P, KB, WG], F32R)
        w_lo = sb(top, "w_lo", [P, KB, WG], F32R)
        x = sb(top, "x", [P, NH, KB, NB])
        ident = sb(top, "ident", [P, P])
        amask = sb(top, "amask", [P, NH, BT])
        amask_t = sb(top, "amask_t", [P, LR])
        idx_sb = sb(top, "idx_sb", [1, NB], I32)

        with ExitStack() as pk:
            th = sb(pk, "th", [P, 2, HG, PA + PB])
            rr = sb(pk, "rr", [P, 2, HG, PA + PB])
            ab = sb(pk, "ab", [P, 2, HG, PA + PB])
            e1 = sb(pk, "e1", [P, 2, HG, PA + PB])
            e2 = sb(pk, "e2", [P, 2, HG, PA])
            gg = sb(pk, "gg", [P, NG, HG, PA + PB])
            small = sb(pk, "small", [P, 28, NH])
            prm_sb = sb(pk, "prm_sb", [P, N_PRM, NH])
            lvec = sb(pk, "lvec", [P, PA + PB])
            sgn = sb(pk, "sgn", [P, 1])
            half_pi = sb(pk, "half_pi", [P, 1])
            zeros = sb(pk, "zeros", [NH, P])
            k_sb = sb(pk, "k_sb", [PA, NG, HG, PB])

        wd_hi = sb(top, "wd_hi", [P, FB, NL + LR], F32R)
        wd_lo = sb(top, "wd_lo", [P, FB, NL + LR], F32R)

        a_gu = sb(top, "a_gu", [P, KB * 2, BT, R])
        a_raw = sb(top, "a_raw", [P, BT, AW])
        b_raw = [sb(top, "b_raw0", [LR, 2 * 512])]

        with ExitStack() as pa:
            toep = sb(pa, "toep", [P, RC, 2, NL])
            um = sb(pa, "um", [P, RC, 2 * KB * NB])
            cv = sb(pa, "cv", [P, 2, 2 * KB * NB])
            len_i = sb(pa, "len_i", [P, NB], I32)
            len_f = sb(pa, "len_f", [P, NB])
            lcol = sb(pa, "lcol", [P, 2, KB])
            lmask = sb(pa, "lmask", [P, 2, KB, NB])
            stage = sb(pa, "stage", [P, RS, 2 * 512])

        b_raw.append(sb(top, "b_raw1", [LR, 2 * 512]))
        bd_raw = sb(top, "bd_raw", [LR, NL])
        b_spl = sb(top, "b_spl", [P, 2, 512], F32R)
        bd_spl = sb(top, "bd_spl", [P, NL], F32R)
        xt = sb(top, "xt", [P, KB, P])
        x_hi = sb(top, "x_hi", [P, 2, KB, P], F32R)
        x_lo = sb(top, "x_lo", [P, 2, KB, P], F32R)
        h_act = sb(top, "h_act", [P, 2, 512])
        y_sb = sb(top, "y_sb", [P, NL])
        t_m = sb(top, "t_m", [P, NH, BT])
        t_hi = sb(top, "t_hi", [P, 2, P], F32R)
        t_lo = sb(top, "t_lo", [P, 2, P], F32R)
        td_m = sb(top, "td_m", [P, 2, LR])
        td_hi = sb(top, "td_hi", [P, P], F32R)
        td_lo = sb(top, "td_lo", [P, P], F32R)
        ht_hi = sb(top, "ht_hi", [P, FB, P], F32R)
        ht_lo = sb(top, "ht_lo", [P, FB, P], F32R)

        ps_g = [top.enter_context(nc.psum_tensor(f"ps_g{i}", [P, 512], F32)) for i in range(2)]
        ps_u = [top.enter_context(nc.psum_tensor(f"ps_u{i}", [P, 512], F32)) for i in range(2)]
        ps_da = top.enter_context(nc.psum_tensor("ps_da", [P, 512], F32))
        ps_db = top.enter_context(nc.psum_tensor("ps_db", [P, 512], F32))
        ps_x = [top.enter_context(nc.psum_tensor(f"ps_x{i}", [P, 512], F32)) for i in range(2)]
        ps_k = [ps_da, ps_db]
        ps_c = [ps_g[0], ps_g[1], ps_u[0], ps_u[1]]

        prm_in, len_in, idx_in = sem("prm_in"), sem("len_in"), sem("idx_in")
        x_in = [sem(f"x_in{g}") for g in range(NG)]
        stage_in = [sem(f"stage_in{i}") for i in range(RS)]
        stage_hi, stage_lo = sem("stage_hi"), sem("stage_lo")
        consts, ident_s, amask_ok, amask_ps, amaskt_ok = (sem("consts"), sem("ident_s"), sem("amask_ok"), sem("amask_ps"),
                                                 sem("amaskt_ok"))
        dar_ok = sem("dar_ok")
        phase_done, mask_done = sem("phase_done"), sem("mask_done")
        steps = sem("steps")
        logmag, mag_done, trig_in, trig_done = sem("logmag"), sem("mag_done"), sem("trig_in"), sem("trig_done")
        ang_in, ang_out, tab_ready = sem("ang_in"), sem("ang_out"), sem("tab_ready")
        k_ps, k_ready, zero_out = sem("k_ps"), sem("k_ready"), sem("zero_out")
        k_out = [sem(f"k_out{g}") for g in range(NG)]
        toep_in = [sem(f"toep_in{i}") for i in range(RC)]
        um_in = [sem(f"um_in{i}") for i in range(RC)]
        um_ready, conv_ps, conv_sb, x1_pool = sem("um_ready"), sem("conv_ps"), sem("conv_sb"), sem("x1_pool")
        x1_dve = sem("x1_dve")
        a_in = sem("a_in")
        ag_ok = sem("ag_ok")
        b_in = [sem("b_in0"), sem("b_in1")]
        bd_in = sem("bd_in")
        b_hi, b_lo = sem("b_hi"), sem("b_lo")
        bd_hi, bd_lo = sem("bd_hi"), sem("bd_lo")
        ad_hi, ad_lo = sem("ad_hi"), sem("ad_lo")
        xt_ok, xhi_ok, xlo_ok = sem("xt_ok"), sem("xhi_ok"), sem("xlo_ok")
        a_ps, tm_ok, thi_ok, tlo_ok = sem("a_ps"), sem("tm_ok"), sem("thi_ok"), sem("tlo_ok")
        g_ps, u_ps, silu_ok, act_ok = sem("g_ps"), sem("u_ps"), sem("silu_ok"), sem("act_ok")
        ht_ps, hthi_ok, htlo_ok = sem("ht_ps"), sem("hthi_ok"), sem("htlo_ok")
        ad_ps = sem("ad_ps")
        res_ps, res_ok = sem("res_ps"), sem("res_ok")
        down_ps, td_ok, td_ps, tdhi_ok, tdlo_ok = (sem("down_ps"), sem("td_ok"), sem("td_ps"), sem("tdhi_ok"),
                                                   sem("tdlo_ok"))
        y_ps, y_ok, y_out = sem("y_ps"), sem("y_ok"), sem("y_out")

        def wait(eng, s, v):
            if not isinstance(v, int) or v > 0:
                eng.wait_ge(s, v)

        def tiles(eng, body):
            body(0, 0, True, False)
            with eng.Fori(0, NT // 2 - 1) as a:
                body(a, 1, False, False)
                body(a + 1, 0, False, False)
            body(NT // 2 - 1, 1, False, True)

        def chunk_uses(a, q, c):
            return NC * a + (NC * q + c) // 2

        pieces = []
        for c in range(NC):
            for kb in range(KB):
                cols = slice(chunk_col(c, 0), chunk_col(c, 0) + 2 * CH[c][1])
                pieces.append((wgu[kb * P:(kb + 1) * P, cols], w_hi[:, kb, cols], w_lo[:, kb, cols], P, (2 * CH[c][1],)))
        for f0 in range(0, FB - 1, 2):
            pieces.append((wd[f0 * P:(f0 + 2) * P, :].rearrange("(g p) n -> p g n", p=P),
                           wd_hi[:, f0:f0 + 2, 0:NL], wd_lo[:, f0:f0 + 2, 0:NL], P, (2, NL)))
        pieces.append((wd[(FB - 1) * P:NF, :], wd_hi[0:FLAST, FB - 1, 0:NL], wd_lo[0:FLAST, FB - 1, 0:NL], FLAST, (NL,)))

        NP_GU = KB * NC

        def staged(n):
            shape = pieces[n][4]
            size = shape[0] * (shape[1] if len(shape) > 1 else 1)
            v = stage[0:pieces[n][3], n % RS, 0:size]
            return v.rearrange("p (g n) -> p g n", g=2) if len(shape) > 1 else v

        DT, NAR, DAR, DAI = 8, 9, 10, 11

        block = top.enter_context(nc.Block())

        @block.sync
        def _(sp):
            def load_piece(n):
                wait(sp, stage_lo, n - RS + 1)
                sp.dma_start(staged(n), pieces[n][0]).then_inc(stage_in[n % RS], 16)

            def load_x(g, half):
                h0, nh = g * HG + half * (HG // 2), HG // 2
                w = KB * NB
                sp.dma_start(x[:, h0:h0 + nh, :, :].rearrange("p h k b -> p (h k b)"),
                             xT[:, h0 * w:(h0 + nh) * w]).then_inc(x_in[g], 16)

            def store_taps(g):
                sp.wait_ge(k_ready, g + 1)
                dst = bass.AP(tensor=kpad, offset=g * HG * (P + NL) + P, ap=[[PB, PA], [P + NL, HG], [1, PB]])
                sp.dma_start(dst, k_sb[:, g, :, :]).then_inc(k_out[g], 16)

            def load_toep(pair, slot, group, first):
                sp.wait_ge(k_out[group], 16)
                if not first:
                    sp.wait_ge(conv_ps, pair - RC + 1)
                src = bass.AP(tensor=kpad, offset=pair * (2 * (P + NL)) + 1, ap=[[1, P], [P + NL, 2], [1, NL]])
                sp.dma_start(toep[:, slot, :, :], src).then_inc(toep_in[slot], 16)

            def load_um(pair, slot, first):
                if not first:
                    sp.wait_ge(conv_ps, pair - RC + 1)
                sp.dma_start(um[:, slot, :], xr[bass.ds(pair * P, P), :]).then_inc(um_in[slot], 16)

            def indices(a, q):
                return [sp.value_load(idx_sb[0:1, bass.ds((2 * a + q) * BT + b, 1)], min_val=0, max_val=15)
                        for b in range(BT)]

            def load_a(a, q, ids):
                wait(sp, ag_ok, 2 * a + q)
                wait(sp, ad_lo, 2 * a + q)
                for b in range(BT):
                    src = atab[bass.ds(ids[b], 1), :, :].rearrange("a p n -> (a p) n")
                    sp.dma_start(a_raw[:, b, :], src).then_inc(a_in, 16)

            sp.dma_start(prm_sb[:, :, :], prm.rearrange("p (a h) -> p a h", a=N_PRM)).then_inc(prm_in, 16)
            load_piece(0)
            load_piece(1)
            sp.dma_start(len_i[:, :], lens.partition_broadcast(P)).then_inc(len_in, 16)
            sp.dma_start(idx_sb[0:1, :], idx.partition_broadcast(1)).then_inc(idx_in, 16)
            sp.wait_ge(consts, 1)
            sp.dma_start(kpad.ap()[:, 0:P], zeros[:, :]).then_inc(zero_out, 16)
            load_piece(2)
            for pair in range(RC):
                load_um(pair, pair, True)
            load_x(0, 0)
            load_x(0, 1)
            load_piece(3)
            load_x(1, 0)
            load_x(1, 1)
            load_piece(4)
            load_x(2, 0)
            load_x(2, 1)
            load_piece(5)
            sp.wait_ge(idx_in, 16)
            ids0 = indices(0, 0)
            store_taps(0)
            load_piece(6)
            sp.wait_ge(zero_out, 16)
            for pair in range(RC):
                load_toep(pair, pair, 0, True)
                if pair % 2:
                    load_piece(7 + pair // 2)
            store_taps(1)
            load_piece(9)
            for pair in range(RC, 2 * RC):
                load_toep(pair, pair % RC, 1, False)
                load_um(pair, pair % RC, False)
            store_taps(2)
            load_x(3, 0)
            for pair in range(2 * RC, PAIRS):
                load_toep(pair, pair % RC, pair // RC, False)
                load_um(pair, pair % RC, False)
                if pair == 2 * RC:
                    store_taps(3)
                if pair == 2 * RC + 2:
                    load_x(3, 1)

            def load_b(a, q, c, ids):
                n = NC * (2 * a + q) + c
                wait(sp, b_lo, 2 * n - 2)
                slot, w = (NC * q + c) % 2, 2 * CH[c][1]
                for b in range(BT):
                    src = btab[bass.ds(ids[b], 1), :, chunk_col(c, 0):chunk_col(c, 0) + w].rearrange("a r n -> (a r) n")
                    sp.dma_start(b_raw[slot][b * R:(b + 1) * R, 0:w], src).then_inc(b_in[slot], 16)

            def load_bd(a, q, ids):
                wait(sp, bd_lo, 2 * a + q)
                for b in range(BT):
                    src = btab[bass.ds(ids[b], 1), :, WG:BW].rearrange("a r n -> (a r) n")
                    sp.dma_start(bd_raw[b * R:(b + 1) * R, :], src).then_inc(bd_in, 16)

            def store(a, q):
                t = 2 * a + q
                sp.wait_ge(y_ok, 2 * t + 2)
                sp.dma_start(out[bass.ds(t * P, P), :], y_sb[:, :]).then_inc(y_out, 16)

            load_a(0, 0, ids0)
            load_piece(10)
            load_piece(11)
            load_b(0, 0, 0, ids0)
            load_piece(NP_GU)
            load_piece(NP_GU + 1)
            load_piece(NP_GU + 2)
            sp.wait_ge(conv_ps, PAIRS - RC + 2)
            load_b(0, 0, 1, ids0)
            load_bd(0, 0, ids0)
            load_piece(NP_GU + 3)
            def body(a, q, first, last):
                load_b(a, q, 2, indices(a, q))
                if first:
                    for n in range(NP_GU + 4, len(pieces)):
                        load_piece(n)
                na, nq = (a, 1) if q == 0 else (a + 1, 0)
                if not last:
                    ids = indices(na, nq)
                    load_b(na, nq, 0, ids)
                if not first:
                    store(*((a, 0) if q == 1 else (a - 1, 1)))
                if not last:
                    load_a(na, nq, ids)
                    load_bd(na, nq, ids)
                    load_b(na, nq, 1, ids)

            tiles(sp, body)
            for half in range(2):
                c = slice(0, DA_W) if half == 0 else slice(DA_W, NL)
                sp.wait_ge(y_ok, 2 * (NT - 1) + half + 1)
                sp.dma_start(out[(NT - 1) * P:NT * P, c], y_sb[:, c]).then_inc(y_out, 16)
            sp.wait_ge(y_out, 16 * (NT + 1))

        @block.gpsimd
        def _(pool):
            nc.gpsimd.memset(zeros[:, :], 0.0).then_inc(consts, 1)
            nc.gpsimd.iota(lvec[:, 0:PA], pattern=[[PB, PA]], base=0, channel_multiplier=0,
                           allow_small_or_imprecise_dtypes=True).then_inc(consts, 1)
            nc.gpsimd.iota(lvec[:, PA:PA + PB], pattern=[[1, PB]], base=0, channel_multiplier=0,
                           allow_small_or_imprecise_dtypes=True).then_inc(consts, 1)
            for i in range(2):
                nc.gpsimd.iota(lcol[:, i, :], pattern=[[P, KB]], base=(P - 1, 0)[i], channel_multiplier=(-1, 1)[i],
                               allow_small_or_imprecise_dtypes=True).then_inc(consts, 1)
            nc.gpsimd.memset(half_pi[:, :], PI / 2).then_inc(consts, 1)
            nc.gpsimd.memset(ident[:, :], 0.0).then_inc(ident_s, 1)
            pool.wait_ge(ident_s, 1)
            nc.gpsimd.affine_select(out=ident[:, :], in_=ident[:, :], compare_op=ALU.not_equal, fill=1.0, base=0,
                                    pattern=[[-1, P]], channel_multiplier=1).then_inc(ident_s, 1)
            nc.gpsimd.memset(amask[:, :, :], SCALE).then_inc(amask_ok, 1)
            pool.wait_ge(amask_ok, 1)
            for h in range(2):
                v = amask[h * LR:(h + 1) * LR, :, :]
                nc.gpsimd.affine_select(out=v, in_=v, compare_op=ALU.is_ge, fill=0.0, base=0,
                                        pattern=[[0, NH], [-R, BT]], channel_multiplier=1).then_inc(amask_ok, 1)
            pool.wait_ge(amask_ok, 3)
            for h in range(2):
                v = amask[h * LR:(h + 1) * LR, :, :]
                nc.gpsimd.affine_select(out=v, in_=v, compare_op=ALU.is_ge, fill=0.0, base=R - 1,
                                        pattern=[[0, NH], [R, BT]], channel_multiplier=-1).then_inc(amask_ok, 1)
            pool.wait_ge(amask_ok, 5)

            def split_lo(n):
                pool.wait_ge(stage_hi, n + 1)
                nc.gpsimd.tensor_tensor(pieces[n][2], staged(n), pieces[n][1].bitcast(F32),
                                        ALU.subtract).then_inc(stage_lo, 1)

            def add_conv(pair):
                pool.wait_ge(conv_sb, pair + 1)
                v = x[:, 2 * pair:2 * pair + 2, :, :].rearrange("p h k b -> p (h k b)")
                nc.gpsimd.tensor_tensor(v, v, cv[:, pair % 2, :], ALU.add).then_inc(x1_pool, 1)

            split_lo(0)
            pool.wait_ge(consts, 6)
            pool.wait_ge(dar_ok, 1)
            for g in range(NG):
                shape = [P, HG, PA + PB]
                nc.gpsimd.tensor_tensor(gg[:, g], small[:, DAR, g * HG:(g + 1) * HG].unsqueeze(2).broadcast_to(shape),
                                        lvec[:, :].unsqueeze(1).broadcast_to(shape), ALU.mult).then_inc(logmag, 1)
            for n in range(1, 10):
                split_lo(n)
            pool.wait_ge(x_in[0], 32)
            for pair in range(RC):
                add_conv(pair)

            def pack_a(t):
                src = a_raw[:, :, 0:KB * 2 * R].rearrange("p b (k r) -> p k b r", r=R)
                nc.gpsimd.tensor_copy(a_gu[:, :, :, :], src).then_inc(ag_ok, 1)

            pool.wait_ge(a_in, 16 * BT)
            pack_a(0)
            for n in range(10, len(pieces)):
                split_lo(n)

            def body(a, q, first, last):
                if not last:
                    t = 2 * a + q + 1
                    pool.wait_ge(res_ps, t)
                    pool.wait_ge(xlo_ok, t)
                    pool.wait_ge(a_ps, t)
                    pool.wait_ge(a_in, 16 * BT * (t + 1))
                    pool.wait_ge(x1_dve, PAIRS - RC)
                    nc.gpsimd.tensor_copy(xt[:, :, :].rearrange("p k (h b) -> p k h b", b=BT),
                                          x[:, :, :, bass.ds(t * BT, BT)].rearrange("p h k b -> p k h b")
                                          ).then_inc(xt_ok, 1)
                    pack_a(t)

            tiles(pool, body)

        @block.scalar
        def _(act):
            def split_hi(n):
                act.wait_ge(stage_in[n % RS], 16 * (n // RS + 1))
                nc.scalar.copy(pieces[n][1], staged(n)).then_inc(stage_hi, 1)

            def trig(g):
                s = g % 2
                act.wait_ge(trig_in, g + 1)
                if g >= 2:
                    act.wait_ge(k_ps, g - 1)
                nc.scalar.activation(e1[0:NM, s, :, :], ab[0:NM, s, :, :], ACT.Sin, bias=half_pi[0:NM, :],
                                     scale=-1.0).then_inc(trig_done, 1)
                nc.scalar.activation(e1[NM:P, s, :, :], rr[NM:P, s, :, :], ACT.Sin).then_inc(trig_done, 1)
                nc.scalar.activation(e2[0:NM, s, :, :], rr[0:NM, s, :, 0:PA], ACT.Sin).then_inc(trig_done, 1)
                nc.scalar.activation(e2[NM:P, s, :, :], ab[NM:P, s, :, 0:PA], ACT.Sin, bias=half_pi[NM:P, :],
                                     scale=-1.0).then_inc(trig_done, 1)

            for n in range(RS):
                split_hi(n)
            act.wait_ge(consts, 6)
            act.wait_ge(ang_in, 1)
            nc.scalar.activation(small[:, 16, :], small[:, 14, :], ACT.Sin).then_inc(ang_out, 1)
            nc.scalar.activation(small[:, 17, :], small[:, 15, :], ACT.Sin, bias=half_pi[:, :],
                                 scale=-1.0).then_inc(ang_out, 1)
            trig(0)
            act.wait_ge(logmag, NG)
            nc.scalar.activation(gg[:, :, :, :], gg[:, :, :, :], ACT.Exp).then_inc(mag_done, 1)
            for n in range(3, 6):
                split_hi(n)
            trig(1)
            split_hi(6)
            split_hi(7)
            trig(2)
            split_hi(8)
            trig(3)
            for n in range(9, NP_GU):
                split_hi(n)
            act.wait_ge(k_ready, NG)
            for g in range(NG):
                act.wait_ge(k_out[g], 16)

            def x_hi_part(a, q, first):
                t = 2 * a + q
                act.wait_ge(xt_ok, t + 1)
                if first:
                    act.wait_ge(conv_ps, PAIRS)
                else:
                    wait(act, u_ps, NC * (t - 1))
                nc.scalar.copy(x_hi[:, q, :, :], xt[:, :, :]).then_inc(xhi_ok, 1)

            def b_hi_part(a, q, c, up):
                n = NC * (2 * a + q) + c
                slot, w = (NC * q + c) % 2, CH[c][1]
                if up == 0:
                    act.wait_ge(b_in[slot], 16 * BT * (chunk_uses(a, q, c) + 1))
                wait(act, u_ps if up else g_ps, n)
                nc.scalar.copy(b_spl[0:LR, up, 0:w], b_raw[slot][:, up * w:(up + 1) * w]).then_inc(b_hi, 1)

            def body(a, q, first, last):
                t = 2 * a + q
                na, nq = (a, 1) if q == 0 else (a + 1, 0)
                act.wait_ge(tm_ok, t + 1)
                wait(act, u_ps, NC * t)
                for up in range(2):
                    src = t_m[up * LR:(up + 1) * LR, :, :].rearrange("p h b -> p (h b)")
                    nc.scalar.copy(t_hi[0:LR, up, :], src).then_inc(thi_ok, 1)
                    nc.scalar.copy(t_hi[LR:P, up, :], src).then_inc(thi_ok, 1)
                if not first:
                    td_hi_part(t - 1)

                def silu(c):
                    n = NC * t + c
                    act.wait_ge(g_ps, n + 1)
                    wait(act, ht_ps, n - 1)
                    s, w = (NC * q + c) % 2, CH[c][1]
                    nc.scalar.activation(h_act[:, s, 0:w], ps_g[s][:, 0:w], ACT.Silu).then_inc(silu_ok, 1)

                def ht_hi_part(c):
                    act.wait_ge(ht_ps, NC * t + c + 1)
                    if c == 0 and first:
                        act.wait_ge(stage_lo, len(pieces))
                    elif c == 0:
                        act.wait_ge(down_ps, t)
                    f0, nf = BLK[c]
                    bank = [0, 1, 1][c]
                    if c < NC - 1:
                        nc.scalar.copy(ht_hi[:, f0:f0 + nf, :],
                                       ps_x[bank][:, 0:nf * P].rearrange("p (f t) -> p f t", t=P)).then_inc(hthi_ok, 1)
                    else:
                        nc.scalar.copy(ht_hi[:, f0:f0 + nf - 1, :],
                                       ps_x[bank][:, 0:(nf - 1) * P].rearrange("p (f t) -> p f t", t=P)).then_inc(hthi_ok, 1)
                        nc.scalar.copy(ht_hi[0:FLAST, f0 + nf - 1, :],
                                       ps_x[bank][0:FLAST, (nf - 1) * P:nf * P]).then_inc(hthi_ok, 1)

                act.wait_ge(a_in, 16 * BT * (t + 1))
                wait(act, down_ps, t)
                ad = a_raw[:, :, KB * 2 * R:AW].rearrange("p b (f r) -> p f b r", r=R)
                nc.scalar.copy(wd_hi[:, :, NL:NL + LR].rearrange("p f (b r) -> p f b r", r=R), ad).then_inc(ad_hi, 1)
                if first:
                    split_hi(NP_GU + 1)
                silu(0)
                if first:
                    split_hi(NP_GU + 2)
                b_hi_part(a, q, 1, 0)
                b_hi_part(a, q, 1, 1)
                act.wait_ge(bd_in, 16 * BT * (t + 1))
                wait(act, y_ps, t)
                nc.scalar.copy(bd_spl[0:LR, :], bd_raw[:, :]).then_inc(bd_hi, 1)
                if first:
                    split_hi(NP_GU + 3)
                silu(1)
                b_hi_part(a, q, 2, 0)
                if first:
                    split_hi(NP_GU + 4)
                    split_hi(NP_GU + 5)
                b_hi_part(a, q, 2, 1)
                ht_hi_part(0)
                silu(2)
                if not last:
                    b_hi_part(na, nq, 0, 0)
                    b_hi_part(na, nq, 0, 1)
                ht_hi_part(1)
                act.wait_ge(res_ps, t + 1)
                wait(act, y_out, 16 * t)
                nc.scalar.copy(y_sb[:, :], ps_x[0][:, :]).then_inc(res_ok, 1)
                if not last:
                    x_hi_part(na, nq, False)
                ht_hi_part(2)

            def td_hi_part(t):
                act.wait_ge(td_ps, t + 1)
                wait(act, y_ps, t)
                nc.scalar.copy(td_hi[:, :], ps_x[1][:, 0:P]).then_inc(tdhi_ok, 1)

            x_hi_part(0, 0, True)
            b_hi_part(0, 0, 0, 0)
            b_hi_part(0, 0, 0, 1)
            split_hi(NP_GU)
            tiles(act, body)
            td_hi_part(NT - 1)

        @block.vector
        def _(dve):
            count = [0]

            def chain(ins, now, beside=None, i=0):
                count[0] += 1
                ins.then_inc(steps, 1)
                if beside is not None:
                    beside(i)
                if now:
                    dve.wait_ge(steps, count[0])

            def step(ins, now=True):
                chain(ins, now)

            def sm(i, n=1):
                return small[:, i:i + n, :]

            V = nc.vector

            def exp_parts(src, at, n, beside=None):
                def step(ins, i):
                    chain(ins, True, beside, i)

                q_, s_, r_, k_ = sm(at, n), sm(at + n, n), sm(at + 2 * n, n), sm(at + 3 * n, n)
                step(V.tensor_scalar(r_, src, 88.0, -87.0, ALU.min, ALU.max), 0)
                step(V.tensor_scalar(s_, r_, LOG2E, MAGIC + 127.0, ALU.mult, ALU.add), 1)
                step(V.tensor_scalar(k_, s_, MAGIC + 127.0, None, ALU.subtract), 2)
                step(V.tensor_scalar(s_.bitcast(I32), s_.bitcast(I32), 23, None, ALU.logical_shift_left), 3)
                step(V.scalar_tensor_tensor(out=r_, in0=k_, scalar=-LN2_HI, in1=r_, op0=ALU.mult, op1=ALU.add), 4)
                step(V.scalar_tensor_tensor(out=r_, in0=k_, scalar=-LN2_LO, in1=r_, op0=ALU.mult, op1=ALU.add), 5)
                step(V.tensor_scalar(q_, r_, 1 / 5040, None, ALU.mult), 6)
                for i, c in enumerate((1 / 720, 1 / 120, 1 / 24, 1 / 6, 1 / 2, 1.0), 7):
                    step(V.scalar_tensor_tensor(out=q_, in0=q_, scalar=c, in1=r_, op0=ALU.add, op1=ALU.mult), i)
                return q_, s_

            def stt(o, i, i0, s, i1, op0, op1):
                step(V.scalar_tensor_tensor(out=sm(o), in0=sm(i0), scalar=s, in1=i1, op0=op0, op1=op1))

            step(V.memset(sgn[0:NM, :], 1.0), False)
            step(V.memset(sgn[NM:P, :], -1.0), False)
            prm_ = lambda i, n=1: prm_sb[:, i:i + n, :]
            dve.wait_ge(prm_in, 16)
            q_, s_ = exp_parts(prm_(0, 2), 0, 2)
            step(V.scalar_tensor_tensor(out=sm(8, 2), in0=q_, scalar=1.0, in1=s_, op0=ALU.add, op1=ALU.mult))
            V.scalar_tensor_tensor(out=sm(DAR), in0=sm(NAR), scalar=-1.0, in1=sm(DT), op0=ALU.mult,
                                   op1=ALU.mult).then_inc(dar_ok, 1)
            step(V.tensor_tensor(sm(DAI), prm_(2), sm(DT), ALU.mult))
            dve.wait_ge(consts, 6)
            def phase_step(g, i):
                s = g % 2
                hs = slice(g * HG, (g + 1) * HG)
                shape = [P, HG, PA + PB]
                t_, r_, a_ = th[:, s], rr[:, s], ab[:, s]
                if i > 0:
                    dve.wait_ge(phase_done, 5 * g + i)
                if i == 0:
                    ins = V.tensor_tensor(r_, small[:, DAI, hs].unsqueeze(2).broadcast_to(shape),
                                          lvec[:, :].unsqueeze(1).broadcast_to(shape), ALU.mult)
                elif i == 1:
                    ins = V.tensor_scalar(t_, r_, 1 / PI, MAGIC, ALU.mult, ALU.add)
                elif i == 2:
                    ins = V.tensor_scalar(a_, t_, MAGIC, None, ALU.subtract)
                elif i == 3:
                    ins = V.scalar_tensor_tensor(out=r_, in0=a_, scalar=-PI_HI, in1=r_, op0=ALU.mult, op1=ALU.add)
                elif i == 4:
                    ins = V.scalar_tensor_tensor(out=r_, in0=a_, scalar=-PI_LO, in1=r_, op0=ALU.mult, op1=ALU.add)
                else:
                    ins = V.tensor_scalar(a_.bitcast(I32), r_.bitcast(I32), ABS_BITS, None, ALU.bitwise_and)
                ins.then_inc(phase_done if i < 5 else trig_in, 1)

            def phases(g, first=0):
                for i in range(first, 6):
                    phase_step(g, i)

            def length_mask_step(i):
                if i == 0:
                    dve.wait_ge(len_in, 16)
                    V.tensor_copy(len_f[:, :], len_i[:, :]).then_inc(mask_done, 1)
                elif i <= 2 * KB:
                    if i == 1:
                        dve.wait_ge(mask_done, 1)
                    side, kb = divmod(i - 1, KB)
                    V.tensor_scalar(lmask[:, side, kb, :], len_f[:, :], lcol[:, side, kb:kb + 1], None,
                                    ALU.is_gt).then_inc(mask_done, 1)

            beside = lambda i: phase_step(0, i)
            chain(V.tensor_scalar(sm(12), sm(DAI), 0.5, None, ALU.mult), True, beside, 0)
            chain(V.tensor_scalar(sm(13), sm(12), 1 / PI, MAGIC, ALU.mult, ALU.add), True, beside, 1)
            chain(V.tensor_scalar(sm(13), sm(13), MAGIC, None, ALU.subtract), True, beside, 2)
            chain(V.scalar_tensor_tensor(out=sm(14), in0=sm(13), scalar=-PI_HI, in1=sm(12), op0=ALU.mult, op1=ALU.add),
                  True, beside, 3)
            chain(V.scalar_tensor_tensor(out=sm(14), in0=sm(13), scalar=-PI_LO, in1=sm(14), op0=ALU.mult, op1=ALU.add),
                  True, beside, 4)
            V.tensor_scalar(sm(15).bitcast(I32), sm(14).bitcast(I32), ABS_BITS, None, ALU.bitwise_and).then_inc(ang_in, 1)
            phase_step(0, 5)
            dve.wait_ge(dar_ok, 1)
            q_, s_ = exp_parts(sm(DAR), 0, 1, length_mask_step)
            step(V.tensor_tensor(sm(4), q_, s_, ALU.mult))
            step(V.scalar_tensor_tensor(out=sm(4), in0=s_, scalar=-1.0, in1=sm(4), op0=ALU.add, op1=ALU.add))
            dve.wait_ge(ang_out, 2)
            SI, CO, EM = 16, 17, 4
            step(V.tensor_tensor(sm(19), sm(SI), sm(SI), ALU.mult))
            step(V.tensor_scalar(sm(20), sm(19), -2.0, 1.0, ALU.mult, ALU.add))
            step(V.tensor_tensor(sm(20), sm(20), sm(EM), ALU.mult))
            step(V.scalar_tensor_tensor(out=sm(20), in0=sm(19), scalar=-2.0, in1=sm(20), op0=ALU.mult, op1=ALU.add))
            step(V.tensor_tensor(sm(21), sm(SI), sm(CO), ALU.mult))
            step(V.tensor_scalar(sm(21), sm(21), 2.0, None, ALU.mult))
            step(V.scalar_tensor_tensor(out=sm(21), in0=sm(EM), scalar=1.0, in1=sm(21), op0=ALU.add, op1=ALU.mult))
            XR, YI = 20, 21
            step(V.tensor_tensor(sm(22), sm(NAR), sm(NAR), ALU.mult), False)
            step(V.tensor_tensor(sm(23), prm_(2), prm_(2), ALU.mult))
            step(V.tensor_tensor(sm(22), sm(22), sm(23), ALU.add))
            step(V.reciprocal(sm(22), sm(22)))
            step(V.tensor_tensor(sm(23), sm(YI), prm_(2), ALU.mult), False)
            step(V.tensor_tensor(sm(24), sm(XR), sm(NAR), ALU.mult))
            step(V.tensor_tensor(sm(23), sm(23), sm(24), ALU.subtract))
            step(V.tensor_tensor(sm(23), sm(23), sm(22), ALU.mult), False)
            step(V.tensor_tensor(sm(24), sm(XR), prm_(2), ALU.mult), False)
            step(V.tensor_tensor(sm(25), sm(YI), sm(NAR), ALU.mult))
            step(V.scalar_tensor_tensor(out=sm(24), in0=sm(24), scalar=-1.0, in1=sm(25), op0=ALU.mult, op1=ALU.subtract))
            step(V.tensor_tensor(sm(24), sm(24), sm(22), ALU.mult))
            step(V.tensor_tensor(sm(25), prm_(3), sm(23), ALU.mult), False)
            step(V.tensor_tensor(sm(26), prm_(4), sm(24), ALU.mult))
            step(V.tensor_tensor(sm(25), sm(25), sm(26), ALU.subtract))
            step(V.tensor_tensor(sm(26), prm_(3), sm(24), ALU.mult), False)
            step(V.tensor_tensor(sm(27), prm_(4), sm(23), ALU.mult))
            step(V.tensor_tensor(sm(26), sm(26), sm(27), ALU.add))
            step(V.tensor_scalar(sm(25), sm(25), sgn[:, :], 2.0, ALU.mult, ALU.mult))
            step(V.tensor_scalar(sm(26), sm(26), -2.0, None, ALU.mult))

            def taps(g):
                dve.wait_ge(k_ps, g + 1)
                step(V.tensor_copy(k_sb[:, g, :, :], ps_k[g % 2][0:PA, 0:HG * PB].rearrange("a (h b) -> a h b", b=PB)))
                V.tensor_tensor(k_sb[0:1, g, :, 0], k_sb[0:1, g, :, 0], prm_sb[0:1, 5, g * HG:(g + 1) * HG],
                                ALU.add).then_inc(k_ready, 1)

            def tables(g):
                s = g % 2
                hs = slice(g * HG, (g + 1) * HG)
                t_, g_, c1, c2 = th[:, s], gg[:, g], e1[:, s], e2[:, s]
                pr = small[:, 25, hs].unsqueeze(2).broadcast_to([P, HG, PA])
                pi_ = small[:, 26, hs].unsqueeze(2).broadcast_to([P, HG, PA])
                step(V.scalar_tensor_tensor(out=g_.bitcast(I32), in0=t_.bitcast(I32), scalar=31, in1=g_.bitcast(I32),
                                            op0=ALU.logical_shift_left, op1=ALU.bitwise_xor))
                dve.wait_ge(trig_done, 4 * g + 4)
                w_ = ab[:, s, :, 0:PA]
                step(V.tensor_tensor(w_, c1[:, :, 0:PA], pr, ALU.mult), False)
                step(V.tensor_tensor(c2, c2, pi_, ALU.mult))
                step(V.tensor_tensor(c2, c2, w_, ALU.add))
                V.tensor_tensor(c2, c2, g_[:, :, 0:PA], ALU.mult).then_inc(tab_ready, 1)
                V.tensor_tensor(c1[:, :, PA:], c1[:, :, PA:], g_[:, :, PA:], ALU.mult).then_inc(tab_ready, 1)

            def two(v):
                return v.rearrange("p (h n) -> p h n", h=2)

            def mask_input(pair, slot):
                dve.wait_ge(um_in[slot], 4 * (pair - slot) + 16)
                V.tensor_tensor(two(um[:, slot, :]), two(um[:, slot, :]), mask_in, ALU.mult).then_inc(um_ready, 1)

            def mask_output(pair, slot):
                dve.wait_ge(conv_ps, pair + 1)
                V.tensor_tensor(two(cv[:, slot % 2, :]), two(ps_c[slot][:, :]), mask_out, ALU.mult).then_inc(conv_sb, 1)

            def add_conv(pair, slot):
                v = x[:, bass.ds(2 * pair, 2), :, :].rearrange("p h k b -> p (h k b)")
                dve.wait_ge(conv_sb, pair + 1)
                V.tensor_tensor(v, v, cv[:, slot % 2, :], ALU.add).then_inc(x1_dve, 1)

            dve.wait_ge(mag_done, 1)
            tables(0)
            mask_in, mask_out = (lmask[:, i, :, :].rearrange("p k b -> p (k b)").unsqueeze(1).broadcast_to([P, 2, KB * NB])
                                 for i in range(2))

            taps(0)
            phases(1)
            dve.wait_ge(mask_done, 2 * KB + 1)
            mask_input(0, 0)
            mask_input(1, 1)
            phases(2)
            tables(1)
            mask_input(2, 2)
            mask_input(3, 3)
            taps(1)
            phases(3)
            tables(2)
            mask_output(0, 0)
            mask_input(4, 0)
            taps(2)
            tables(3)
            mask_input(5, 1)
            mask_output(1, 1)
            taps(3)
            for pair in (2, 3):
                dve.wait_ge(x1_pool, pair - 1)
                mask_output(pair, pair)
            mask_input(6, 2)
            dve.wait_ge(x1_pool, RC)
            for g in range(1, NG - 1):
                dve.wait_ge(x_in[g], 32)
            with dve.Fori(1, NG - 1) as j:
                for i in range(RC):
                    mask_output(RC * j + i, i)
                    mask_input(RC * j + i + 3, (i + 3) % RC)
                    add_conv(RC * j + i, i)
            dve.wait_ge(x_in[NG - 1], 32)
            for pair in range(PAIRS - RC, PAIRS):
                mask_output(pair, pair % RC)
                if pair + 3 < PAIRS:
                    mask_input(pair + 3, (pair + 3) % RC)
                add_conv(pair, pair % RC)
            dve.wait_ge(x1_dve, PAIRS - RC)
            V.tensor_copy(xt[:, :, :].rearrange("p k (h b) -> p k h b", b=BT),
                          x[:, :, :, 0:BT].rearrange("p h k b -> p k h b")).then_inc(xt_ok, 1)
            dve.wait_ge(amask_ps, 1)
            V.tensor_copy(amask_t[:, :], ps_x[0][:, 0:LR]).then_inc(amaskt_ok, 1)

            def x_lo_part(a, q, first):
                t = 2 * a + q
                dve.wait_ge(xhi_ok, t + 1)
                V.tensor_tensor(x_lo[:, q, :, :], xt[:, :, :], x_hi[:, q, :, :].bitcast(F32),
                                ALU.subtract).then_inc(xlo_ok, 1)

            def b_lo_part(a, q, c, up):
                n = NC * (2 * a + q) + c
                slot, w = (NC * q + c) % 2, CH[c][1]
                dve.wait_ge(b_hi, 2 * n + up + 1)
                V.tensor_tensor(b_spl[LR:P, up, 0:w], b_raw[slot][:, up * w:(up + 1) * w],
                                b_spl[0:LR, up, 0:w].bitcast(F32), ALU.subtract).then_inc(b_lo, 1)

            def td_lo_part(t):
                dve.wait_ge(tdhi_ok, t + 1)
                V.tensor_tensor(td_lo[:, :], ps_x[1][:, 0:P], td_hi[:, :].bitcast(F32), ALU.subtract).then_inc(tdlo_ok, 1)

            def finish(t):
                dve.wait_ge(y_ps, t + 1)
                dve.wait_ge(res_ok, t + 1)
                V.tensor_tensor(y_sb[:, 0:DA_W], y_sb[:, 0:DA_W], ps_da[:, 0:DA_W], ALU.add).then_inc(y_ok, 1)
                V.tensor_tensor(y_sb[:, DA_W:NL], y_sb[:, DA_W:NL], ps_db[:, 0:DB_W], ALU.add).then_inc(y_ok, 1)

            def body(a, q, first, last):
                t = 2 * a + q
                na, nq = (a, 1) if q == 0 else (a + 1, 0)
                dve.wait_ge(a_ps, t + 1)
                wait(dve, tlo_ok, 4 * t)
                V.tensor_tensor(t_m[:, :, :], ps_x[0][:, 0:P].rearrange("p (h b) -> p h b", b=BT), amask[:, :, :],
                                ALU.mult).then_inc(tm_ok, 1)
                dve.wait_ge(thi_ok, 4 * t + 4)
                for up in range(2):
                    rows = slice(up * LR, (up + 1) * LR)
                    src = t_m[rows, :, :].rearrange("p h b -> p (h b)")
                    for half in range(2):
                        V.tensor_tensor(t_lo[half * LR:(half + 1) * LR, up, :], src, t_hi[rows, up, :].bitcast(F32),
                                        ALU.subtract).then_inc(tlo_ok, 1)
                if not first:
                    td_lo_part(t - 1)

                def gated(c):
                    n = NC * t + c
                    s, w = (NC * q + c) % 2, CH[c][1]
                    dve.wait_ge(silu_ok, n + 1)
                    dve.wait_ge(u_ps, n + 1)
                    V.tensor_tensor(h_act[:, s, 0:w], h_act[:, s, 0:w], ps_u[s][:, 0:w], ALU.mult).then_inc(act_ok, 1)

                def ht_lo_part(c):
                    f0, nf = BLK[c]
                    bank = [0, 1, 1][c]
                    dve.wait_ge(hthi_ok, (NC + 1) * t + c + 1 + (c == NC - 1))
                    full = nf if c < NC - 1 else nf - 1
                    V.tensor_tensor(ht_lo[:, f0:f0 + full, :],
                                    ps_x[bank][:, 0:full * P].rearrange("p (f t) -> p f t", t=P),
                                    ht_hi[:, f0:f0 + full, :].bitcast(F32), ALU.subtract).then_inc(htlo_ok, 1)
                    if full < nf:
                        V.tensor_tensor(ht_lo[0:FLAST, f0 + full, :], ps_x[bank][0:FLAST, full * P:nf * P],
                                        ht_hi[0:FLAST, f0 + full, :].bitcast(F32), ALU.subtract).then_inc(htlo_ok, 1)

                dve.wait_ge(ad_hi, t + 1)
                ad = a_raw[:, :, KB * 2 * R:AW].rearrange("p b (f r) -> p f b r", r=R)
                cols = lambda w: w[:, :, NL:NL + LR].rearrange("p f (b r) -> p f b r", r=R)
                V.tensor_tensor(cols(wd_lo), ad, cols(wd_hi).bitcast(F32), ALU.subtract).then_inc(ad_lo, 1)
                b_lo_part(a, q, 1, 0)
                gated(0)
                b_lo_part(a, q, 1, 1)
                if not first:
                    finish(t - 1)
                dve.wait_ge(bd_hi, t + 1)
                V.tensor_tensor(bd_spl[LR:P, :], bd_raw[:, :], bd_spl[0:LR, :].bitcast(F32),
                                ALU.subtract).then_inc(bd_lo, 1)
                b_lo_part(a, q, 2, 0)
                gated(1)
                b_lo_part(a, q, 2, 1)
                ht_lo_part(0)
                if not last:
                    b_lo_part(na, nq, 0, 0)
                gated(2)
                if not last:
                    b_lo_part(na, nq, 0, 1)
                ht_lo_part(1)
                if not last:
                    x_lo_part(na, nq, False)
                ht_lo_part(2)
                dve.wait_ge(ad_ps, t + 1)
                wait(dve, td_ps, t)
                both = lambda v: v.unsqueeze(1).broadcast_to([P, 2, LR])
                V.tensor_tensor(td_m[:, :, :], both(ps_db[:, DB_W:DB_W + LR]), both(amask_t[:, :]),
                                ALU.mult).then_inc(td_ok, 1)

            x_lo_part(0, 0, True)
            b_lo_part(0, 0, 0, 0)
            b_lo_part(0, 0, 0, 1)
            dve.wait_ge(amaskt_ok, 1)
            tiles(dve, body)
            td_lo_part(NT - 1)
            finish(NT - 1)

        @block.tensor
        def _(pe):
            T = nc.tensor
            def taps(g):
                s = g % 2
                pe.wait_ge(tab_ready, 2 * g + 2)
                if g >= 2:
                    pe.wait_ge(k_ready, g - 1)
                for h in range(HG):
                    last = T.matmul(ps_k[s][0:PA, h * PB:(h + 1) * PB], e2[:, s, h, :], e1[:, s, h, PA:PA + PB],
                                    start=True, stop=True)
                last.then_inc(k_ps, 1)

            def conv(pair, slot, first):
                pe.wait_ge(toep_in[slot], 4 * (pair - slot) + 16)
                pe.wait_ge(um_ready, pair + 1)
                if not first:
                    pe.wait_ge(conv_sb, pair - RC + 1)
                for h in range(2):
                    at = h * KB * NB
                    for d in range(KB):
                        n = (KB - d) * NB
                        last = T.matmul(ps_c[slot][:, at + d * NB:at + KB * NB], toep[:, slot, h, d * P:(d + 1) * P],
                                        um[:, slot, at:at + n], start=(d == 0), stop=(d == KB - 1))
                last.then_inc(conv_ps, 1)

            taps(0)
            conv(0, 0, True)
            taps(1)
            conv(1, 1, True)
            conv(2, 2, True)
            conv(3, 3, True)
            taps(2)
            conv(4, 0, False)
            taps(3)
            with pe.Fori(1, NG - 1) as j:
                for i in range(1, RC + 1):
                    conv(RC * j + i, i % RC, False)
            for pair in range(PAIRS - RC + 1, PAIRS):
                conv(pair, pair % RC, False)
            pe.wait_ge(amask_ok, 5)
            pe.wait_ge(ident_s, 2)
            T.transpose(ps_x[0][:, 0:LR], amask[0:LR, :, :].rearrange("p h b -> p (h b)"),
                        ident[0:LR, 0:LR]).then_inc(amask_ps, 1)
            def body(a, q, first, last):
                t = 2 * a + q
                pe.wait_ge(ag_ok, t + 1)
                pe.wait_ge(xt_ok, t + 1)
                wait(pe, res_ok, t)
                if first:
                    pe.wait_ge(amaskt_ok, 1)
                for kb in range(KB):
                    w = a_gu[:, 2 * kb:2 * kb + 2, :, :].rearrange("p g b r -> p (g b r)")
                    ins = T.matmul(ps_x[0][:, 0:P], w, xt[:, kb, :], start=(kb == 0), stop=(kb == KB - 1))
                ins.then_inc(a_ps, 1)

                def base(c, up):
                    n = NC * t + c
                    s, w = (NC * q + c) % 2, CH[c][1]
                    ps = (ps_u if up else ps_g)[s]
                    col = chunk_col(c, up)
                    if first and not up:
                        pe.wait_ge(stage_lo, KB * (c + 1))
                    if c == 0 and not up:
                        pe.wait_ge(xlo_ok, t + 1)
                    if not up:
                        wait(pe, act_ok, n - 1)
                    for kb in range(KB):
                        for xs, ws in ((x_hi, w_hi), (x_hi, w_lo), (x_lo, w_hi)):
                            T.matmul(ps[:, 0:w], xs[:, q, kb, :], ws[:, kb, col:col + w],
                                     start=(kb == 0 and xs is x_hi and ws is w_hi), stop=False)

                def lora(c, up):
                    n = NC * t + c
                    s, w = (NC * q + c) % 2, CH[c][1]
                    ps = (ps_u if up else ps_g)[s]
                    if c == 0 and not up:
                        pe.wait_ge(tlo_ok, 4 * t + 4)
                    pe.wait_ge(b_lo, 2 * n + up + 1)
                    T.matmul(ps[:, 0:w], t_hi[:, up, :], b_spl[:, up, 0:w], start=False, stop=False)
                    T.matmul(ps[:, 0:w], t_lo[:, up, :], b_spl[:, up, 0:w], start=False,
                             stop=True).then_inc(u_ps if up else g_ps, 1)

                def transpose_act(c):
                    f0, nf = BLK[c]
                    s = (NC * q + c) % 2
                    bank = [0, 1, 1][c]
                    pe.wait_ge(act_ok, NC * t + c + 1)
                    if c == 0:
                        pe.wait_ge(tm_ok, t + 1)
                    elif c == 1:
                        wait(pe, tdlo_ok, t)
                    else:
                        pe.wait_ge(htlo_ok, (NC + 1) * t + 2)
                    for f in range(nf):
                        rows = P if f0 + f < FB - 1 else FLAST
                        ins = T.transpose(ps_x[bank][0:rows, f * P:(f + 1) * P], h_act[:, s, f * P:f * P + rows],
                                          ident[:, :])
                    ins.then_inc(ht_ps, 1)

                def down(f, bank):
                    rows = P if f < FB - 1 else FLAST
                    ps, c0, c1 = ((ps_da, 0, DA_W), (ps_db, DA_W, NL + LR))[bank]
                    for hs, ws in ((ht_hi, wd_hi), (ht_hi, wd_lo), (ht_lo, wd_hi)):
                        ins = T.matmul(ps[:, 0:c1 - c0], hs[0:rows, f, :], ws[0:rows, f, c0:c1],
                                       start=(f == 0 and hs is ht_hi and ws is wd_hi),
                                       stop=(bank == 1 and f == FB - 1 and hs is ht_lo))
                    return ins

                def down_chunk(c):
                    for f in range(BLK[c][0], BLK[c][0] + BLK[c][1]):
                        for bank in range(2):
                            down(f, bank)

                base(0, 0)
                if not first:
                    transpose_td(t - 1)
                lora(0, 0)
                base(0, 1)
                lora(0, 1)
                if not first:
                    down_lora(t - 1)
                for up in range(2):
                    base(1, up)
                    lora(1, up)
                transpose_act(0)
                for up in range(2):
                    base(2, up)
                    lora(2, up)
                transpose_act(1)
                pe.wait_ge(htlo_ok, (NC + 1) * t + 1)
                for kb in range(KB):
                    ins = T.transpose(ps_x[0][:, kb * P:(kb + 1) * P], xt[:, kb, :], ident[:, :])
                ins.then_inc(res_ps, 1)
                wait(pe, y_ok, 2 * t)
                if first:
                    pe.wait_ge(stage_lo, len(pieces))
                pe.wait_ge(ad_lo, t + 1)
                down_chunk(0)
                transpose_act(2)
                pe.wait_ge(htlo_ok, (NC + 1) * t + 2)
                down_chunk(1)
                pe.wait_ge(htlo_ok, (NC + 1) * (t + 1))
                for f in range(BLK[2][0], FB):
                    ins = down(f, 1)
                ins.then_inc(ad_ps, 1)
                for f in range(BLK[2][0], FB):
                    ins = down(f, 0)
                ins.then_inc(down_ps, 1)

            def transpose_td(t):
                pe.wait_ge(td_ok, t + 1)
                pe.wait_ge(htlo_ok, (NC + 1) * (t + 1))
                T.transpose(ps_x[1][:, 0:P], td_m[:, :, :].rearrange("p a r -> p (a r)"), ident[:, :]).then_inc(td_ps, 1)

            def down_lora(t):
                pe.wait_ge(tdlo_ok, t + 1)
                pe.wait_ge(bd_lo, t + 1)
                for ts, end in ((td_hi, False), (td_lo, True)):
                    T.matmul(ps_da[:, 0:DA_W], ts[:, :], bd_spl[:, 0:DA_W], start=False, stop=end)
                    ins = T.matmul(ps_db[:, 0:DB_W], ts[:, :], bd_spl[:, DA_W:NL], start=False, stop=end,
                                   skip_group_check=True)
                ins.then_inc(y_ps, 1)

            tiles(pe, body)
            transpose_td(NT - 1)
            down_lora(NT - 1)


def kernel(x, itok_B_8_3872, itok_B_2_6, L0_cond_log_dt, L0_cond_C, L0_cond_log_A_real, L0_cond_A_imag, L0_cond_D,
           L1_cond_W_gate, L1_cond_W_up, L1_cond_W_down, L1_cond_A_gate, L1_cond_B_gate, L1_cond_A_up, L1_cond_B_up,
           L1_cond_A_down, L1_cond_B_down):
    import numpy as np
    import concourse.bacc as bacc
    from concourse.bass_utils import run_bass_kernel_spmd

    xT = np.asarray(x).reshape(NB, NH, KB, P).transpose(3, 1, 2, 0).reshape(P, NH * KB * NB)

    xr = xT.reshape(P, NH // 2, 2 * KB * NB)[::-1].transpose(1, 0, 2).reshape(NH // 2 * P, 2 * KB * NB)

    def interleave(g, u):
        return np.concatenate([m[..., s:s + w] for s, w in CH for m in (g, u)], axis=-1)

    wgu = interleave(np.asarray(L1_cond_W_gate).T, np.asarray(L1_cond_W_up).T)
    wd = np.asarray(L1_cond_W_down).T
    b_gu = interleave(np.asarray(L1_cond_B_gate)[0].transpose(0, 2, 1), np.asarray(L1_cond_B_up)[0].transpose(0, 2, 1))
    b_d = np.asarray(L1_cond_B_down)[0].transpose(0, 2, 1)
    btab = np.concatenate([b_gu, b_d], axis=-1)
    n_ad = btab.shape[0]
    a_g = np.asarray(L1_cond_A_gate)[0].reshape(n_ad, R, KB, P)
    a_u = np.asarray(L1_cond_A_up)[0].reshape(n_ad, R, KB, P)
    a_gu = np.stack([a_g, a_u], axis=1).transpose(0, 4, 3, 1, 2).reshape(n_ad, P, KB * 2 * R)
    a_dn = np.asarray(L1_cond_A_down)[0]
    a_dn = np.concatenate([a_dn, np.zeros((n_ad, R, FB * P - NF), a_dn.dtype)], axis=-1)
    a_dn = a_dn.reshape(n_ad, R, FB, P).transpose(0, 3, 2, 1).reshape(n_ad, P, FB * R)
    atab = np.concatenate([a_gu, a_dn], axis=-1)
    C = np.asarray(L0_cond_C)
    per_mode = [np.asarray(L0_cond_log_A_real).T, np.asarray(L0_cond_A_imag).T, C[..., 0].T, C[..., 1].T]
    rows = [np.broadcast_to(np.asarray(L0_cond_log_dt), (NM, NH))] + per_mode + [
        np.broadcast_to(np.asarray(L0_cond_D), (NM, NH))]
    half = np.concatenate(rows, axis=1)
    prm = np.concatenate([half, half], axis=0)

    arrays = {"xT": xT, "xr": xr, "wgu": wgu, "wd": wd, "atab": atab, "btab": btab, "prm": prm,
              "lens": np.asarray(itok_B_8_3872), "idx": np.asarray(itok_B_2_6)}
    arrays = {k: np.ascontiguousarray(v) for k, v in arrays.items()}
    nc = bacc.Bacc("TRN2", target_bir_lowering=False, num_devices=1, dynamic_dma_scratch_size=1024)
    ins = [nc.dram_tensor(k, v.shape, mybir.dt.from_np(v.dtype), kind="ExternalInput").ap() for k, v in arrays.items()]
    out = nc.dram_tensor("out", (NT * P, NL), F32, kind="ExternalOutput").ap()
    program(nc, *ins, out)
    r = run_bass_kernel_spmd(nc, [arrays], core_ids=[0])
    y = r.results[0]["out"].reshape(NT, NH, BT, NL).transpose(0, 2, 1, 3).reshape(NB, NH, NL)
    return y
```
